# Optimizing a Trainium2 kernel written in Bass

```python
import numpy as np
import jax
import jax.numpy as jnp

def _softmax(x, axis=-1):
    return jax.nn.softmax(x, axis=axis)

def _gelu(x):
    return jax.nn.gelu(x, approximate=True)

def _silu(x):
    return jax.nn.silu(x)

def _sigmoid(x):
    return jax.nn.sigmoid(x)

def _layernorm(x, axis=-1, eps=1e-05):
    m = jnp.mean(x, axis=axis, keepdims=True)
    v = jnp.var(x, axis=axis, keepdims=True)
    return (x - m) / jnp.sqrt(v + eps)

def _scatter_add(tgt, idx, src, axis=0):
    return tgt.at[idx].add(src)

def _segment_sum(src, seg, n):
    return jax.ops.segment_sum(src, seg, n)
kernel_name = 'mk_flamingo_gated_d1_seqx_r8_243b42'

def setup_inputs(seed: int=0):
    np.random.seed(seed)
    _w = jnp.asarray

    def _rec_inputs():
        import jax
        import jax.numpy as jnp
        _rk = jax.random.key(seed)
        x = -0.0003929 + 0.9999 * jax.random.normal(jax.random.fold_in(_rk, 1), (8, 128, 512), jnp.float32)
        _lenS = 128 - jax.random.randint(jax.random.fold_in(_rk, 7), (8,), 0, max(1, 128 // 4) + 1, jnp.int32)
        _lenS2 = 128 - jax.random.randint(jax.random.fold_in(_rk, 8), (8,), 0, max(1, 128 // 4) + 1, jnp.int32)
        _ctx_4096P = jax.random.normal(jax.random.fold_in(_rk, 11), (8, 16, 512), jnp.float32)
        _ctx_4096c = jax.random.dirichlet(jax.random.fold_in(_rk, 511), 0.3 * jnp.ones((16,), jnp.float32), (8, 128))
        _ctx_4096t = jnp.einsum('bsk,bkd->bsd', _ctx_4096c, _ctx_4096P)
        _ctx_4096t = _ctx_4096t * jax.lax.rsqrt(jnp.mean(jnp.square(_ctx_4096t)) + 1e-12) * 0.953939
        ctx_4096 = 2.81802e-05 + 1.00001 * (_ctx_4096t + 0.3 * jax.random.normal(jax.random.fold_in(_rk, 611), (8, 128, 512), jnp.float32))
        _g = jax.random.normal(jax.random.fold_in(_rk, 9001), (2, 1), jnp.float32)
        _g = jnp.sign(_g) * jnp.maximum(jnp.abs(_g), 1.0) + (_g == 0) * 1.0
        g_xattn = _g[0]
        g_ffn = _g[1]
        return (x, ctx_4096, g_xattn, g_ffn)
    x, ctx_4096, g_xattn, g_ffn = _rec_inputs()

    def _L0_xattn_setup():
        import jax, jax.numpy as jnp
        import numpy as np
        EMBED = 512
        NUM_Q = 32
        NUM_KV = 8
        GROUPS = NUM_Q // NUM_KV
        HEAD_DIM = EMBED // NUM_Q
        KV_DIM = HEAD_DIM * NUM_KV
        key = jax.random.key(seed)
        ks = jax.random.split(key, 12)
        B, S = (2, 256)
        s = 0.02
        return {'query': jax.random.normal(ks[0], (B, S, EMBED), jnp.float32), 'key': jax.random.normal(ks[1], (B, S, EMBED), jnp.float32), 'value': jax.random.normal(ks[2], (B, S, EMBED), jnp.float32), 'Wq': jax.random.normal(ks[3], (EMBED, EMBED), jnp.float32) * s, 'bq': jnp.zeros((EMBED,), jnp.float32), 'Wk': jax.random.normal(ks[4], (EMBED, KV_DIM), jnp.float32) * s, 'bk': jnp.zeros((KV_DIM,), jnp.float32), 'Wv': jax.random.normal(ks[5], (EMBED, KV_DIM), jnp.float32) * s, 'bv': jnp.zeros((KV_DIM,), jnp.float32), 'Wo': jax.random.normal(ks[6], (EMBED, EMBED), jnp.float32) * s, 'bo': jnp.zeros((EMBED,), jnp.float32)}
    _L0_xattn_all = _L0_xattn_setup()
    _L0_xattn_in = {k: v for k, v in _L0_xattn_all.items() if k in ('Wq', 'bq', 'Wk', 'bk', 'Wv', 'bv', 'Wo', 'bo')}
    del _L0_xattn_all

    def _L0_ffn_setup():
        import jax, jax.numpy as jnp
        import numpy as np
        BS = 128
        FP8_MAX = 448.0

        def act_quant(x):
            T, K = x.shape
            xb = x.reshape(T, K // BS, BS)
            amax = jnp.max(jnp.abs(xb), axis=-1)
            scale = amax / FP8_MAX + 1e-12
            xq = (xb / scale[:, :, None]).reshape(T, K)
            return (xq, scale)

        def linear_dsv3(x, wq, w_scale):
            T, K = x.shape
            N = wq.shape[0]
            xq, xs = act_quant(x)
            xdq = (xq.reshape(T, K // BS, BS) * xs[:, :, None]).reshape(T, K)
            wdq = (wq.reshape(N // BS, BS, K // BS, BS) * w_scale[:, None, :, None]).reshape(N, K)
            return xdq @ wdq.T
        key = jax.random.key(seed)
        ks = jax.random.split(key, 4)
        DIM, INTER = (512, 1792)

        def make_qweight(k, n, m):
            w = jax.random.normal(k, (n, m), dtype=jnp.float32) * 0.02
            wb = w.reshape(n // BS, BS, m // BS, BS)
            amax = jnp.max(jnp.abs(wb), axis=(1, 3))
            scale = amax / FP8_MAX + 1e-12
            wq = (wb / scale[:, None, :, None]).reshape(n, m)
            return (wq, scale)
        x = jax.random.normal(ks[0], (2, 128, DIM), dtype=jnp.float32)
        w1, w1_scale = make_qweight(ks[1], INTER, DIM)
        w3, w3_scale = make_qweight(ks[2], INTER, DIM)
        w2, w2_scale = make_qweight(ks[3], DIM, INTER)
        return {'x': x, 'w1': w1, 'w1_scale': w1_scale, 'w3': w3, 'w3_scale': w3_scale, 'w2': w2, 'w2_scale': w2_scale}
    _L0_ffn_all = _L0_ffn_setup()
    _L0_ffn_in = {k: v for k, v in _L0_ffn_all.items() if k in ('w1', 'w1_scale', 'w3', 'w3_scale', 'w2', 'w2_scale')}
    del _L0_ffn_all
    return {'x': x, 'ctx_4096': ctx_4096, 'g_xattn': g_xattn, 'g_ffn': g_ffn, 'L0_xattn_Wq': _L0_xattn_in['Wq'], 'L0_xattn_bq': _L0_xattn_in['bq'], 'L0_xattn_Wk': _L0_xattn_in['Wk'], 'L0_xattn_bk': _L0_xattn_in['bk'], 'L0_xattn_Wv': _L0_xattn_in['Wv'], 'L0_xattn_bv': _L0_xattn_in['bv'], 'L0_xattn_Wo': _L0_xattn_in['Wo'], 'L0_xattn_bo': _L0_xattn_in['bo'], 'L0_ffn_w1': _L0_ffn_in['w1'], 'L0_ffn_w1_scale': _L0_ffn_in['w1_scale'], 'L0_ffn_w3': _L0_ffn_in['w3'], 'L0_ffn_w3_scale': _L0_ffn_in['w3_scale'], 'L0_ffn_w2': _L0_ffn_in['w2'], 'L0_ffn_w2_scale': _L0_ffn_in['w2_scale']}

def reference(x, ctx_4096, g_xattn, g_ffn, L0_xattn_Wq, L0_xattn_bq, L0_xattn_Wk, L0_xattn_bk, L0_xattn_Wv, L0_xattn_bv, L0_xattn_Wo, L0_xattn_bo, L0_ffn_w1, L0_ffn_w1_scale, L0_ffn_w3, L0_ffn_w3_scale, L0_ffn_w2, L0_ffn_w2_scale):
    import jax
    import jax.numpy as jnp

    def _L0_xattn_ref(query, key, value, Wq, bq, Wk, bk, Wv, bv, Wo, bo):
        import jax, jax.numpy as jnp
        import numpy as np
        EMBED = 512
        NUM_Q = 32
        NUM_KV = 8
        GROUPS = NUM_Q // NUM_KV
        HEAD_DIM = EMBED // NUM_Q
        KV_DIM = HEAD_DIM * NUM_KV
        B, S, _ = query.shape
        Q = query @ Wq + bq
        K = key @ Wk + bk
        V = value @ Wv + bv
        Q = Q.reshape(B, S, NUM_KV, GROUPS, HEAD_DIM).transpose(0, 2, 3, 1, 4)
        K = K.reshape(B, S, NUM_KV, HEAD_DIM).transpose(0, 2, 1, 3)
        V = V.reshape(B, S, NUM_KV, HEAD_DIM).transpose(0, 2, 1, 3)
        scale = 1.0 / jnp.sqrt(jnp.asarray(HEAD_DIM, query.dtype))
        scores = jnp.einsum('bhgqd,bhkd->bhgqk', Q, K) * scale
        w = jax.nn.softmax(scores, axis=-1)
        y = jnp.einsum('bhgqk,bhkd->bhgqd', w, V)
        y = y.transpose(0, 3, 1, 2, 4).reshape(B, S, EMBED)
        return y @ Wo + bo

    def _L0_ffn_ref(x, w1, w1_scale, w3, w3_scale, w2, w2_scale):
        import jax, jax.numpy as jnp
        import numpy as np
        BS = 128
        FP8_MAX = 448.0

        def act_quant(x):
            T, K = x.shape
            xb = x.reshape(T, K // BS, BS)
            amax = jnp.max(jnp.abs(xb), axis=-1)
            scale = amax / FP8_MAX + 1e-12
            xq = (xb / scale[:, :, None]).reshape(T, K)
            return (xq, scale)

        def linear_dsv3(x, wq, w_scale):
            T, K = x.shape
            N = wq.shape[0]
            xq, xs = act_quant(x)
            xdq = (xq.reshape(T, K // BS, BS) * xs[:, :, None]).reshape(T, K)
            wdq = (wq.reshape(N // BS, BS, K // BS, BS) * w_scale[:, None, :, None]).reshape(N, K)
            return xdq @ wdq.T
        B, S, D = x.shape
        xf = x.reshape(-1, D)
        g = linear_dsv3(xf, w1, w1_scale)
        u = linear_dsv3(xf, w3, w3_scale)
        h = jax.nn.silu(g) * u
        y = linear_dsv3(h, w2, w2_scale)
        return y.reshape(B, S, D)
    x = x + jnp.tanh(g_xattn[0]) * _L0_xattn_ref(_layernorm(x, axis=-1), ctx_4096, ctx_4096, L0_xattn_Wq, L0_xattn_bq, L0_xattn_Wk, L0_xattn_bk, L0_xattn_Wv, L0_xattn_bv, L0_xattn_Wo, L0_xattn_bo)
    x = x + jnp.tanh(g_ffn[0]) * _L0_ffn_ref(_layernorm(x, axis=-1), L0_ffn_w1, L0_ffn_w1_scale, L0_ffn_w3, L0_ffn_w3_scale, L0_ffn_w2, L0_ffn_w2_scale)
    return x

_drawn_inputs = setup_inputs


def setup_inputs(seed=0):
    import zlib

    import numpy as np

    out = dict(_drawn_inputs(seed))
    spreads = {'L0_xattn_bq': (0.0, 0.8),
     'L0_xattn_bk': (0.0, 0.8),
     'L0_xattn_bv': (0.0, 0.1),
     'L0_xattn_bo': (0.0, 0.1)}
    factors = {'L0_xattn_Wq': 8.0,
     'L0_xattn_Wk': 8.0,
     'L0_ffn_w1_scale': 7.311,
     'L0_ffn_w3_scale': 7.106,
     'L0_ffn_w2_scale': 8.0}
    for name, (base, spread) in spreads.items():
        noise = np.random.default_rng([zlib.crc32(name.encode()), seed]).standard_normal(out[name].shape)
        drawn = base * np.exp(spread * noise) if base else spread * noise
        out[name] = jnp.asarray(drawn.astype(out[name].dtype))
    for name, factor in factors.items():
        out[name] = (out[name] * factor).astype(out[name].dtype)
    return out
```

```python
from contextlib import ExitStack

import concourse.bass as bass
from concourse import mybir

F32 = mybir.dt.float32
F32R = mybir.dt.float32r
F16 = mybir.dt.float16
BF16 = mybir.dt.bfloat16
ALU = mybir.AluOpType
ACT = mybir.ActivationFunctionType
AX = mybir.AxisListType

P = 128
NBATCH = 8
DM = 512
KB = DM // P
HEADS = 32
KVH = 8
GJ = HEADS // KVH
DH = DM // HEADS
KVD = KVH * DH
PAIRS = KVH // 2
ROWS = 96
VC = 3 * DH + 1
FF = 1792
NCH = FF // P
HALVES = 2
HT = NBATCH // HALVES
TOK = HT * P
W13 = 2 * KB * P
CW = W13 + DM
NSC = CW // P
CHUNKS = HALVES * NCH
EPS = 1e-5
SCALE = DH ** -0.5

KV0, Q0, O0 = 0, KB * 2 * KVD, KB * 2 * KVD + KB * DM
PW = O0 + KB * DM
BQ, BK, BO = 0, DM, DM + 2 * KVD
GATE, SC = BO + DM, BO + DM + 2
SMALL = SC + NCH * NSC


def build(nc, x, ctxt, wproj, small, wff, out):
    with ExitStack() as ctx:
        def sb(name, shape, dt=F32):
            return ctx.enter_context(nc.sbuf_tensor(name, shape, dt))

        def sem(name):
            return ctx.enter_context(nc.semaphore(name))

        def need(eng, s, n):
            if isinstance(n, int) and n <= 0:
                return
            eng.wait_ge(s, n)

        def r32(ap):
            return ap.bitcast(F32)

        X = sb("X", [P, NBATCH, DM])
        x2H = sb("x2H", [P, KB, NBATCH * P], F32R)
        x2L = sb("x2L", [P, KB, NBATCH * P], F32R)
        raw = sb("raw", [P, PW])
        smallrow = sb("smallrow", [P, SMALL])
        tg = sb("tg", [P, 2])
        ident = sb("ident", [P, P])
        w13H = sb("w13H", [P, 2, W13], F32R)
        w13L = sb("w13L", [P, 2, W13], F32R)
        ps = ctx.enter_context(nc.psum_tensor("ps", [P, 8, 512], F32))
        W0, W1, W2, PVB = (ps[:, 4 + i, :] for i in range(4))

        att = ctx.enter_context(ExitStack())

        def sa(name, shape, dt=F32):
            return att.enter_context(nc.sbuf_tensor(name, shape, dt))

        WpH = sa("WpH", [P, PW], F32R)
        WpL = sa("WpL", [P, PW], F32R)
        botg = sa("botg", [P, DM])
        neghalf = sa("neghalf", [P, 1])
        sel = sa("sel", [P, 2, P])
        ct = sa("ct", [P, DM])
        ctH = sa("ctH", [P, DM], F32R)
        ctL = sa("ctL", [P, DM], F32R)
        st1 = sa("st1", [P, 6])
        mv1 = sa("mv1", [P, 2])
        ve1 = sa("ve1", [P, 1])
        rs1 = sa("rs1", [P, 1])
        st2 = sa("st2", [P, 6])
        mv2 = sa("mv2", [P, 2])
        ve2 = sa("ve2", [P, 1])
        rs2 = sa("rs2", [P, 1])
        xn = sa("xn", [P, DM])
        xTH = sa("xTH", [P, DM], F32R)
        xTL = sa("xTL", [P, DM], F32R)
        Qf = sa("Qf", [P, DM])
        KVf = sa("KVf", [P, 2 * KVD])
        Qtok = sa("Qtok", [P, PAIRS * GJ, 3, 32], F32R)
        Ktok = sa("Ktok", [P, PAIRS, 2, 3, 2, DH], F32R)
        Qst = sa("Qst", [P, PAIRS, GJ * P], F32R)
        Kst = sa("Kst", [P, PAIRS, 2, P], F32R)
        mx = sa("mx", [P, PAIRS * GJ, 2])
        Mtok = sa("Mtok", [P, PAIRS * GJ, 32])
        MT = sa("MT", [P, PAIRS, GJ * P])
        v1f = sa("v1f", [P, KVD])
        Vp = sa("Vp", [P, NBATCH, KVH, VC + 1], BF16)
        E = sa("E", [P, 2, GJ * P])
        PH = sa("PH", [P, 3, GJ * P], F16)
        PL = sa("PL", [P, 3, GJ * P], F16)
        osum = sa("osum", [P, HEADS, DH])
        rden = sa("rden", [P, HEADS])
        on = sa("on", [P, HEADS, DH])
        aTH = sa("aTH", [P, DM], F32R)
        aTL = sa("aTL", [P, DM], F32R)
        x2n = sa("x2n", [P, DM])
        att.close()

        w2H = sb("w2H", [P, 2, DM], F32R)
        w2L = sb("w2L", [P, 2, DM], F32R)
        T = sb("T", [P, 2, TOK])
        A = sb("A", [P, 2, TOK])
        hf = sb("hf", [P, 2, TOK])
        hH = sb("hH", [P, 2, TOK], F32R)
        hL = sb("hL", [P, 2, TOK], F32R)

        small_in, wkv_in, wq_in, wo_in = sem("small_in"), sem("wkv_in"), sem("wq_in"), sem("wo_in")
        x_in, ct_in = sem("x_in"), sem("ct_in")
        raw_in = [sem("raw_in0"), sem("raw_in1")]
        consts = sem("consts")
        zeros = sem("zeros")
        selrows = sem("selrows")
        tanhg = sem("tanhg")
        botg_ok = sem("botg_ok")
        wpH_ok, wpL_ok, woL_ok = sem("wpH_ok"), sem("wpL_ok"), sem("woL_ok")
        stats1, mean1, ve1_ok, rs1_ok, xn_ok = (sem(n) for n in ("stats1", "mean1", "ve1_ok", "rs1_ok", "xn_ok"))
        stats2, mean2, ve2_ok, rs2_ok, x2n_ok = (sem(n) for n in ("stats2", "mean2", "ve2_ok", "rs2_ok", "x2n_ok"))
        xbo_ok = sem("xbo_ok")
        ctH_ok, ctL_ok = sem("ctH_ok"), sem("ctL_ok")
        xT_ps, xTH_ok, xTL_ok = sem("xT_ps"), sem("xTH_ok"), sem("xTL_ok")
        kv_ps, kvf_ok, q_ps, qf_ok = sem("kv_ps"), sem("kvf_ok"), sem("q_ps"), sem("qf_ok")
        qtokH, qtokL, ktokH, ktokL = sem("qtokH"), sem("qtokL"), sem("ktokH"), sem("ktokL")
        vparts, vres = sem("vparts"), sem("vres")
        kst_ps, kst_ok, qst_ps, qst_ok = sem("kst_ps"), sem("kst_ok"), sem("qst_ps"), sem("qst_ok")
        s_ps, max_ok, mH_ok, mL_ok = sem("s_ps"), sem("max_ok"), sem("mH_ok"), sem("mL_ok")
        mT_ok, mrows = sem("mT_ok"), sem("mrows")
        st_ps, exp_ok, pH_ok, pL_ok = sem("st_ps"), sem("exp_ok"), sem("pH_ok"), sem("pL_ok")
        pv_ps, pv_read, on_ok = sem("pv_ps"), sem("pv_read"), sem("on_ok")
        aT_ps, aTH_ok, aTL_ok = sem("aT_ps"), sem("aTH_ok"), sem("aTL_ok")
        o_ps, x2_ok = sem("o_ps"), sem("x2_ok")
        x2T_ps, x2H_ok, x2L_ok = sem("x2T_ps"), sem("x2H_ok"), sem("x2L_ok")
        scaled = sem("scaled")
        w13H_ok, w13L_ok, w2H_ok, w2L_ok = sem("w13H_ok"), sem("w13L_ok"), sem("w2H_ok"), sem("w2L_ok")
        g_ps, u_ps, t_ok, a_ok, h_ok, hH_ok, hL_ok = (sem(n) for n in ("g_ps", "u_ps", "t_ok", "a_ok", "h_ok", "hH_ok", "hL_ok"))
        y_used = sem("y_used")
        y_ps, fin_ok, out_done = sem("y_ps"), sem("fin_ok"), sem("out_done")

        block = ctx.enter_context(nc.Block())

        def attention(eng, step):
            step(-1, True, False, False)
            step(0, True, True, False)
            with eng.Fori(1, NBATCH - 1) as i:
                step(i, True, True, True)
            step(NBATCH - 1, False, True, True)
            step(NBATCH, False, False, True)

        def raw_slot(s):
            return raw[:, s * CW:(s + 1) * CW]

        @block.sync
        def _(sp):
            sp.dma_start(xn[:], x[0]).then_inc(x_in, 16)
            sp.dma_start(smallrow[:], small.broadcast_to([P, SMALL])).then_inc(small_in, 16)
            sp.dma_start(raw[:, Q0:O0], wproj[:, Q0:O0]).then_inc(wq_in, 16)
            sp.dma_start(raw[:, O0:PW], wproj[:, O0:PW]).then_inc(wo_in, 16)
            with sp.Fori(1, NBATCH) as b:
                sp.wait_ge(xT_ps, b)
                sp.dma_start(xn[:], x[b]).then_inc(x_in, 16)
                sp.wait_ge(ctL_ok, b)
                sp.dma_start(ct[:], ctxt[b]).then_inc(ct_in, 16)
            sp.wait_ge(wpL_ok, 2)
            sp.wait_ge(woL_ok, 1)
            for c in range(2):
                sp.dma_start(raw_slot(c), wff[c]).then_inc(raw_in[c], 16)
            for h in range(HALVES):
                with sp.Fori(1 - h, NCH // 2) as p:
                    for s in range(2):
                        c = h * NCH + 2 * p + s
                        sp.wait_ge(w2L_ok, c - 1)
                        sp.dma_start(raw_slot(s), wff[2 * p + s]).then_inc(raw_in[s], 16)
                if h == 0:
                    pass
            for t in range(NBATCH):
                sp.wait_ge(fin_ok, t + 1)
                sp.dma_start(out[t], X[:, t, :]).then_inc(out_done, 16)
            sp.wait_ge(out_done, 16 * NBATCH)

        @block.gpsimd
        def _(pool):
            pool.memset(ident[:], 0.0).then_inc(consts, 1)
            pool.memset(sel[:], 1.0).then_inc(consts, 1)
            pool.memset(neghalf[:], -0.5).then_inc(consts, 1)
            pool.memset(Vp[:], 1.0).then_inc(consts, 1)
            pool.wait_ge(consts, 4)
            pool.affine_select(out=ident[:], in_=ident[:], compare_op=ALU.not_equal, fill=1.0, base=0,
                               pattern=[[-1, P]], channel_multiplier=1).then_inc(consts, 1)
            pool.affine_select(out=sel[:], in_=sel[:], compare_op=ALU.is_ge, fill=0.0, base=-ROWS,
                               pattern=[[-2, 2], [0, P]], channel_multiplier=1).then_inc(consts, 1)
            pool.wait_ge(consts, 6)
            pool.affine_select(out=sel[:], in_=sel[:], compare_op=ALU.is_ge, fill=0.0, base=ROWS + 1,
                               pattern=[[2, 2], [0, P]], channel_multiplier=-1).then_inc(consts, 1)

            def step(i, front, back, late):
                f, b = i + 1, i
                if front:
                    pool.wait_ge(botg_ok, 1)
                    pool.wait_ge(x_in, 16 * (f + 1))
                    pool.tensor_tensor(X[:, f, :], xn[:], botg[:], ALU.add).then_inc(xbo_ok, 1)
                    need(pool, xn_ok, f)
                    pool.wait_ge(ve1_ok, f + 1)
                    pool.tensor_tensor(rs1[:], ve1[:], neghalf[:], ALU.pow).then_inc(rs1_ok, 1)
                    pool.wait_ge(ctH_ok, f + 1)
                    need(pool, kv_ps, f)
                    pool.tensor_tensor(ctL[:], ct[:], r32(ctH[:]), ALU.subtract).then_inc(ctL_ok, 1)

                def pl(g):
                    pool.wait_ge(pH_ok, 8 * b + g + 1)
                    pool.tensor_tensor(PL[:, g % 3, :], E[:, g % 2, :], PH[:, g % 3, :],
                                       ALU.subtract).then_inc(pL_ok, 1)
                if back:
                    for g in range(4):
                        pl(g)
                if front:
                    pool.wait_ge(ktokH, 2 * f + 2)
                    need(pool, kst_ps, 2 * f)
                    for gg in range(2):
                        pool.tensor_tensor(Ktok[:, :, gg, 2, gg, :],
                                           KVf[:, 0:KVD].rearrange("p (a g d) -> p a g d", a=PAIRS, g=2)[:, :, gg, :],
                                           r32(Ktok[:, :, gg, 0, gg, :]), ALU.subtract).then_inc(ktokL, 1)
                if back:
                    for g in range(4, 8):
                        pl(g)
                if front:
                    pool.wait_ge(qtokH, f + 1)
                    need(pool, qst_ps, 4 * f)
                    pool.tensor_tensor(Qtok[:, :, 1, :], Qf[:].rearrange("p (a d) -> p a d", d=32),
                                       r32(Qtok[:, :, 0, :]), ALU.subtract).then_inc(qtokL, 1)
                if back:
                    need(pool, x2n_ok, b)
                    pool.wait_ge(ve2_ok, b + 1)
                    pool.tensor_tensor(rs2[:], ve2[:], neghalf[:], ALU.pow).then_inc(rs2_ok, 1)

            pool.wait_ge(wpH_ok, 3)
            pool.tensor_tensor(WpL[:, O0:PW], raw[:, O0:PW], r32(WpH[:, O0:PW]), ALU.subtract).then_inc(woL_ok, 1)
            attention(pool, step)

            for h in range(HALVES):
                with pool.Fori(0, NCH // 2) as p:
                    for s in range(2):
                        n = 2 * p + s
                        pool.wait_ge(raw_in[s], 16 * (h * (NCH // 2) + p + 1))
                        pool.tensor_tensor(
                            raw_slot(s).rearrange("p (a n) -> p a n", n=P), raw_slot(s).rearrange("p (a n) -> p a n", n=P),
                            smallrow[:, bass.ds(SC + n * NSC, NSC)].unsqueeze(2).broadcast_to([P, NSC, P]),
                            ALU.mult).then_inc(scaled, 1)

        @block.scalar
        def _(act):
            act.dma_start(ct[:], ctxt[0]).then_inc(ct_in, 16)
            act.dma_start(raw[:, KV0:Q0], wproj[:, KV0:Q0]).then_inc(wkv_in, 16)
            act.wait_ge(small_in, 16)
            act.activation(tg[:], smallrow[:, GATE:GATE + 2], ACT.Tanh).then_inc(tanhg, 1)
            for s, a, z in ((wkv_in, KV0, Q0), (wq_in, Q0, O0), (wo_in, O0, PW)):
                act.wait_ge(s, 16)
                act.activation(WpH[:, a:z], raw[:, a:z], ACT.Copy).then_inc(wpH_ok, 1)

            def step(i, front, back, late):
                f, b, l = i + 1, i, i - 1
                if front:
                    act.wait_ge(ct_in, 16 * (f + 1))
                    need(act, kv_ps, f)
                    act.activation(ctH[:], ct[:], ACT.Copy).then_inc(ctH_ok, 1)

                def exps(g):
                    act.wait_ge(st_ps, 8 * b + g + 1)
                    need(act, pL_ok, 8 * b + g - 1)
                    act.activation(E[:, g % 2, :], ps[:, g % 4, :], ACT.Exp, scale=SCALE).then_inc(exp_ok, 1)
                if back:
                    exps(0)
                    exps(1)
                if late:
                    act.wait_ge(x2T_ps, l + 1)
                    act.activation(x2H[:, :, bass.ds(l * P, P)], W2.rearrange("p (k n) -> p k n", k=KB),
                                   ACT.Copy).then_inc(x2H_ok, 1)
                if back:
                    exps(2)
                if front:
                    act.wait_ge(xT_ps, f + 1)
                    need(act, q_ps, f)
                    act.activation(xTH[:], W0, ACT.Copy).then_inc(xTH_ok, 1)
                if back:
                    exps(3)
                    exps(4)
                if front:
                    act.wait_ge(kvf_ok, f + 1)
                    need(act, kst_ps, 2 * f)
                    need(act, ktokL, 2 * f)
                    for gg in range(2):
                        act.activation(Ktok[:, :, gg, 0:2, gg, :],
                                       KVf[:, 0:KVD].rearrange("p (a g d) -> p a g d", a=PAIRS, g=2)[:, :, gg, :]
                                       .unsqueeze(2).broadcast_to([P, PAIRS, 2, DH]), ACT.Copy).then_inc(ktokH, 1)
                if back:
                    exps(5)
                if front:
                    act.wait_ge(qf_ok, f + 1)
                    need(act, qst_ps, 4 * f)
                    need(act, qtokL, f)
                    act.activation(Qtok[:, :, 0:3:2, :], Qf[:].rearrange("p (a d) -> p a d", d=32)
                                   .unsqueeze(2).broadcast_to([P, PAIRS * GJ, 2, 32]), ACT.Copy).then_inc(qtokH, 1)
                if back:
                    exps(6)
                    exps(7)
                if front:
                    for a in range(PAIRS):
                        act.wait_ge(qst_ps, 4 * f + a + 1)
                        need(act, st_ps, 8 * f)
                        act.activation(Qst[0:ROWS, a, :], (W0, W1, W2, W0)[a][0:ROWS, :], ACT.Copy).then_inc(qst_ok, 1)
                if back:
                    act.wait_ge(aT_ps, b + 1)
                    need(act, o_ps, b)
                    act.activation(aTH[:], W1, ACT.Copy).then_inc(aTH_ok, 1)
                if front:
                    act.wait_ge(mT_ok, 4 * f + 4)
                    act.activation(Qst[ROWS:P, 2:4, :], MT[ROWS:P, 2:4, :], ACT.Copy).then_inc(mrows, 1)

            attention(act, step)

            def split13(c, s):
                act.wait_ge(scaled, c + 1)
                need(act, u_ps, c - 1)
                act.activation(w13H[:, s, :], raw_slot(s)[:, 0:W13], ACT.Copy).then_inc(w13H_ok, 1)

            def ffn(c, s, ahead):
                if ahead:
                    split13(c + 1, 1 - s)
                act.wait_ge(g_ps, c + 1)
                need(act, a_ok, c - 1)
                act.activation(T[:, s, :], (W0, W2)[s], ACT.Tanh, scale=0.5).then_inc(t_ok, 1)
                need(act, y_used, c - 1)
                act.activation(w2H[:, s, :], raw_slot(s)[:, W13:CW], ACT.Copy).then_inc(w2H_ok, 1)
                act.wait_ge(h_ok, c + 1)
                act.activation(hH[:, s, :], hf[:, s, :], ACT.Copy).then_inc(hH_ok, 1)

            split13(0, 0)
            ffn(0, 0, True)
            ffn(1, 1, True)
            with act.Fori(1, CHUNKS // 2 - 1) as p:
                ffn(2 * p, 0, True)
                ffn(2 * p + 1, 1, True)
            ffn(CHUNKS - 2, 0, True)
            ffn(CHUNKS - 1, 1, False)

        @block.vector
        def _(dve):
            dve.memset(r32(Ktok[:]), 0.0).then_inc(zeros, 1)
            dve.memset(Mtok[:], 0.0).then_inc(zeros, 1)
            dve.wait_ge(consts, 7)
            dve.tensor_copy(Kst[ROWS:P, :, :, :], sel[ROWS:P, :, :].unsqueeze(1).broadcast_to([P - ROWS, PAIRS, 2, P])).then_inc(selrows, 1)
            dve.wait_ge(small_in, 16)
            dve.wait_ge(tanhg, 1)
            dve.tensor_scalar(botg[:], smallrow[:, BO:BO + DM], tg[:, 0:1], None, ALU.mult).then_inc(botg_ok, 1)

            def norm1(f):
                dve.wait_ge(x_in, 16 * (f + 1))
                dve.bn_stats(st1[:], xn[:]).then_inc(stats1, 1)

            def norm1_mean(f):
                dve.bn_aggr(mv1[:], st1[:]).then_inc(mean1, 1)
                dve.wait_ge(mean1, f + 1)
                need(dve, rs1_ok, f)
                dve.tensor_scalar(ve1[:], mv1[:, 1:2], EPS, None, ALU.add).then_inc(ve1_ok, 1)

            def norm1_apply(f):
                dve.wait_ge(rs1_ok, f + 1)
                dve.wait_ge(xbo_ok, f + 1)
                dve.tensor_scalar(xn[:], xn[:], mv1[:, 0:1], rs1[:, 0:1], ALU.subtract, ALU.mult).then_inc(xn_ok, 1)

            def step(i, front, back, late):
                f, b, l = i + 1, i, i - 1

                def p_high(g):
                    dve.wait_ge(exp_ok, 8 * b + g + 1)
                    need(dve, pv_ps, 8 * b + g - 2)
                    dve.tensor_copy(PH[:, g % 3, :], E[:, g % 2, :]).then_inc(pH_ok, 1)

                def pv_sum(q):
                    n = 4 * b + q
                    dve.wait_ge(pv_ps, 8 * b + 2 * q + 2)
                    need(dve, on_ok, 4 * b + q - 3)
                    v = PVB[:, 0:8 * VC].rearrange("p (h c) -> p h c", c=VC)
                    dve.tensor_reduce(osum[:, 8 * q:8 * q + 8, :],
                                      v[:, :, 0:3 * DH].rearrange("p h (t d) -> p h d t", t=3), AX.X, ALU.add).then_inc(pv_read, 1)
                    dve.reciprocal(rden[:, 8 * q:8 * q + 8], v[:, :, 3 * DH]).then_inc(pv_read, 1)
                    dve.wait_ge(pv_read, 2 * n + 2)
                    need(dve, aT_ps, b)
                    dve.tensor_tensor(on[:, 8 * q:8 * q + 8, :], osum[:, 8 * q:8 * q + 8, :],
                                      rden[:, 8 * q:8 * q + 8].unsqueeze(2).broadcast_to([P, 8, DH]), ALU.mult).then_inc(on_ok, 1)

                if front:
                    norm1(f)
                    dve.wait_ge(stats1, f + 1)
                if back:
                    p_high(0)
                if front:
                    norm1_mean(f)
                    norm1_apply(f)
                if back:
                    p_high(1)
                    p_high(2)
                if late:
                    dve.wait_ge(x2H_ok, l + 1)
                    dve.tensor_tensor(x2L[:, :, bass.ds(l * P, P)], W2.rearrange("p (k n) -> p k n", k=KB),
                                      r32(x2H[:, :, bass.ds(l * P, P)]), ALU.subtract).then_inc(x2L_ok, 1)
                if front:
                    dve.wait_ge(xTH_ok, f + 1)
                    dve.tensor_tensor(xTL[:], W0, r32(xTH[:]), ALU.subtract).then_inc(xTL_ok, 1)
                if back:
                    p_high(3)
                if front:
                    dve.wait_ge(kv_ps, f + 1)
                    need(dve, ktokL, 2 * f)
                    need(dve, vparts, 4 * f)
                    dve.tensor_tensor(KVf[:], W1[:, 0:2 * KVD], smallrow[:, BK:BK + 2 * KVD], ALU.add).then_inc(kvf_ok, 1)
                if back:
                    p_high(4)
                    pv_sum(0)
                    p_high(5)
                if front:
                    dve.wait_ge(q_ps, f + 1)
                    need(dve, qtokL, f)
                    dve.tensor_tensor(Qf[:], W0, smallrow[:, BQ:BQ + DM], ALU.add).then_inc(qf_ok, 1)
                    dve.wait_ge(kvf_ok, f + 1)
                    v = KVf[:, KVD:2 * KVD].rearrange("p (g d) -> p g d", g=KVH)
                    w = v1f[:].rearrange("p (g d) -> p g d", g=KVH)
                    vp = Vp[:, f, :, :]
                    dve.tensor_copy(vp[:, :, 0:DH], v).then_inc(vparts, 1)
                    dve.wait_ge(vparts, 4 * f + 1)
                    dve.tensor_tensor(w, v, vp[:, :, 0:DH], ALU.subtract).then_inc(vres, 1)
                    dve.wait_ge(vres, 2 * f + 1)
                    dve.tensor_copy(vp[:, :, DH:2 * DH], w).then_inc(vparts, 1)
                    dve.wait_ge(vparts, 4 * f + 2)
                    dve.tensor_tensor(w, w, vp[:, :, DH:2 * DH], ALU.subtract).then_inc(vres, 1)
                    dve.wait_ge(vres, 2 * f + 2)
                    dve.tensor_copy(vp[:, :, 2 * DH:3 * DH], w).then_inc(vparts, 2)
                if back:
                    p_high(6)
                    pv_sum(1)
                    p_high(7)
                    pv_sum(2)
                if front:
                    for a in range(2):
                        dve.wait_ge(kst_ps, 2 * f + a + 1)
                        need(dve, st_ps, 8 * f)
                        dve.tensor_copy(Kst[0:ROWS, 2 * a:2 * a + 2, :, :],
                                        (W1, W2)[a][0:ROWS, :].rearrange("p (a g k) -> p a g k", a=2, g=2)).then_inc(kst_ok, 1)
                if back:
                    pv_sum(3)
                    dve.wait_ge(aTH_ok, b + 1)
                    dve.tensor_tensor(aTL[:], W1, r32(aTH[:]), ALU.subtract).then_inc(aTL_ok, 1)

                def maxima(a):
                    dve.wait_ge(s_ps, 4 * f + a + 1)
                    need(dve, mL_ok, f)
                    pair = 2 * (a % 2)
                    dve.tensor_reduce(mx[:, 4 * a:4 * a + 4, :],
                                      ps[:, pair:pair + 2, :].rearrange("p b (j g k) -> p (b j) g k", j=2, g=2),
                                      AX.X, ALU.max).then_inc(max_ok, 1)
                if front:
                    maxima(0)
                    maxima(1)
                if back:
                    dve.wait_ge(o_ps, b + 1)
                    dve.wait_ge(xbo_ok, b + 1)
                    need(dve, x2T_ps, b)
                    dve.scalar_tensor_tensor(out=x2n[:], in0=W2, scalar=tg[:, 0:1], in1=X[:, b, :],
                                             op0=ALU.mult, op1=ALU.add).then_inc(x2_ok, 1)
                    dve.wait_ge(x2_ok, 2 * b + 1)
                    dve.bn_stats(st2[:], x2n[:]).then_inc(stats2, 1)
                    dve.tensor_copy(X[:, b, :], x2n[:]).then_inc(x2_ok, 1)
                    dve.wait_ge(stats2, b + 1)
                if front:
                    maxima(2)
                if back:
                    dve.bn_aggr(mv2[:], st2[:]).then_inc(mean2, 1)
                    dve.wait_ge(mean2, b + 1)
                    need(dve, rs2_ok, b)
                    dve.tensor_scalar(ve2[:], mv2[:, 1:2], EPS, None, ALU.add).then_inc(ve2_ok, 1)
                if front:
                    maxima(3)
                    dve.wait_ge(max_ok, 4 * f + 4)
                    need(dve, mrows, 2 * f)
                    hl = Mtok[:, :, 0:4].rearrange("p a (g t) -> p a g t", t=2)
                    dve.tensor_scalar(hl[:, :, :, 0].bitcast(F32R), mx[:], -1.0, None, ALU.mult).then_inc(mH_ok, 1)
                    dve.wait_ge(mH_ok, f + 1)
                    dve.scalar_tensor_tensor(out=hl[:, :, :, 1], in0=mx[:], scalar=-1.0, in1=hl[:, :, :, 0],
                                             op0=ALU.mult, op1=ALU.subtract).then_inc(mL_ok, 1)
                    dve.wait_ge(mL_ok, f + 1)
                    need(dve, mrows, 2 * f)
                    rows = MT[ROWS:P, :, :].rearrange("p a (j q) -> p (a j) q", j=GJ)
                    for q in range(4):
                        dve.transpose(rows[:, :, 32 * q:32 * q + 32], Mtok[32 * q:32 * q + 32, :, :]).then_inc(mT_ok, 1)
                    dve.wait_ge(mT_ok, 4 * f + 4)
                    need(dve, st_ps, 8 * f)
                    dve.tensor_copy(Qst[ROWS:P, 0:2, :], MT[ROWS:P, 0:2, :]).then_inc(mrows, 1)
                if back:
                    dve.wait_ge(rs2_ok, b + 1)
                    dve.wait_ge(x2_ok, 2 * b + 2)
                    dve.tensor_scalar(x2n[:], x2n[:], mv2[:, 0:1], rs2[:, 0:1], ALU.subtract, ALU.mult).then_inc(x2n_ok, 1)

            dve.wait_ge(zeros, 2)
            for n, (a, z) in enumerate(((KV0, Q0), (Q0, O0))):
                dve.wait_ge(wpH_ok, n + 1)
                dve.tensor_tensor(WpL[:, a:z], raw[:, a:z], r32(WpH[:, a:z]), ALU.subtract).then_inc(wpL_ok, 1)
            attention(dve, step)

            def split13(c, s):
                dve.wait_ge(w13H_ok, c + 1)
                dve.tensor_tensor(w13L[:, s, :], raw_slot(s)[:, 0:W13], r32(w13H[:, s, :]), ALU.subtract).then_inc(w13L_ok, 1)

            def final(h):
                for t in range(HT):
                    n = h * HT + t
                    dve.wait_ge(y_ps, n + 1)
                    dve.scalar_tensor_tensor(out=X[:, n, :], in0=ps[:, t, :], scalar=tg[:, 1:2], in1=X[:, n, :],
                                             op0=ALU.mult, op1=ALU.add).then_inc(fin_ok, 1)

            def ffn(c, s, ahead, finish=None):
                if ahead:
                    split13(c + 1, 1 - s)
                if finish is not None:
                    final(finish)
                dve.wait_ge(t_ok, c + 1)
                need(dve, h_ok, c - 1)
                dve.scalar_tensor_tensor(out=A[:, s, :], in0=T[:, s, :], scalar=1.0, in1=(W0, W2)[s],
                                         op0=ALU.add, op1=ALU.mult).then_inc(a_ok, 1)
                dve.wait_ge(u_ps, c + 1)
                dve.wait_ge(a_ok, c + 1)
                need(dve, hL_ok, c - 1)
                dve.scalar_tensor_tensor(out=hf[:, s, :], in0=A[:, s, :], scalar=0.5, in1=(W1, PVB)[s],
                                         op0=ALU.mult, op1=ALU.mult).then_inc(h_ok, 1)
                dve.wait_ge(w2H_ok, c + 1)
                dve.tensor_tensor(w2L[:, s, :], raw_slot(s)[:, W13:CW], r32(w2H[:, s, :]), ALU.subtract).then_inc(w2L_ok, 1)
                dve.wait_ge(hH_ok, c + 1)
                dve.tensor_tensor(hL[:, s, :], hf[:, s, :], r32(hH[:, s, :]), ALU.subtract).then_inc(hL_ok, 1)

            split13(0, 0)
            ffn(0, 0, True)
            ffn(1, 1, True)
            with dve.Fori(1, NCH // 2) as p:
                ffn(2 * p, 0, True)
                ffn(2 * p + 1, 1, True)
            ffn(NCH, 0, True, finish=0)
            ffn(NCH + 1, 1, True)
            with dve.Fori(NCH // 2 + 1, NCH - 1) as p:
                ffn(2 * p, 0, True)
                ffn(2 * p + 1, 1, True)
            ffn(CHUNKS - 2, 0, True)
            ffn(CHUNKS - 1, 1, False)
            final(1)

        @block.tensor
        def _(pe):
            def three(out_ap, aH, aL, bH, bL, start, stop):
                pe.matmul(out_ap, aH, bH, start=start, stop=False)
                pe.matmul(out_ap, aH, bL, start=False, stop=False)
                return pe.matmul(out_ap, aL, bH, start=False, stop=stop)

            def turn(out_ap, in_ap):
                return pe.matmul(out_ap, in_ap, ident[:], start=True, stop=True, is_transpose=True)

            def step(i, front, back, late):
                f, b, l = i + 1, i, i - 1

                def scores_t(g):
                    pe.wait_ge(mrows, 2 * b + 2)
                    need(pe, exp_ok, 8 * b + g - 3)
                    pe.matmul(ps[:, g % 4, :], Kst[:, g // 2, g % 2, :], Qst[:, g // 2, :],
                              start=True, stop=True).then_inc(st_ps, 1)

                def values(g):
                    pe.wait_ge(pL_ok, 8 * b + g + 1)
                    if g == 0:
                        pe.wait_ge(vparts, 4 * b + 3)
                    if g % 2 == 0:
                        need(pe, pv_read, 2 * (4 * b + g // 2))
                    for j in range(GJ):
                        h = (g % 2) * GJ + j
                        o = PVB[:, h * VC:(h + 1) * VC]
                        v = Vp[:, b, g, 0:VC]
                        pe.matmul(o, PH[:, g % 3, j * P:(j + 1) * P], v, start=True, stop=False)
                        m = pe.matmul(o, PL[:, g % 3, j * P:(j + 1) * P], v, start=False, stop=True)
                    m.then_inc(pv_ps, 1)

                if back:
                    scores_t(0)
                    scores_t(1)
                if late:
                    pe.wait_ge(x2n_ok, l + 1)
                    for k in range(KB):
                        m = turn(W2[:, k * P:(k + 1) * P], x2n[:, k * P:(k + 1) * P])
                    m.then_inc(x2T_ps, 1)
                if back:
                    scores_t(2)
                    values(0)
                if front:
                    pe.wait_ge(xn_ok, f + 1)
                    need(pe, qst_ok, 4 * f)
                    for k in range(KB):
                        m = turn(W0[:, k * P:(k + 1) * P], xn[:, k * P:(k + 1) * P])
                    m.then_inc(xT_ps, 1)
                if back:
                    scores_t(3)
                    values(1)
                if front:
                    pe.wait_ge(ctL_ok, f + 1)
                    need(pe, aTL_ok, b)
                    if not isinstance(f, int) or f == 0:
                        pe.wait_ge(wpL_ok, 1)
                    for k in range(KB):
                        c = slice(KV0 + k * 2 * KVD, KV0 + (k + 1) * 2 * KVD)
                        m = three(W1[:, 0:2 * KVD], ctH[:, k * P:(k + 1) * P], ctL[:, k * P:(k + 1) * P],
                                  WpH[:, c], WpL[:, c], k == 0, k == KB - 1)
                    m.then_inc(kv_ps, 1)
                if back:
                    scores_t(4)
                    values(2)
                if front:
                    pe.wait_ge(xTL_ok, f + 1)
                    pe.wait_ge(wpL_ok, 2)
                    for k in range(KB):
                        c = slice(Q0 + k * DM, Q0 + (k + 1) * DM)
                        m = three(W0, xTH[:, k * P:(k + 1) * P], xTL[:, k * P:(k + 1) * P],
                                  WpH[:, c], WpL[:, c], k == 0, k == KB - 1)
                    m.then_inc(q_ps, 1)
                if back:
                    for g in range(5, 8):
                        scores_t(g)
                        values(g - 2)
                    values(6)
                    values(7)
                if front:
                    pe.wait_ge(ktokL, 2 * f + 2)
                    for a in range(2):
                        if a == 1:
                            need(pe, x2L_ok, i)
                        for t in range(4):
                            m = turn((W1, W2)[a][0:ROWS, t * P:(t + 1) * P],
                                     r32(Ktok[:, 2 * a + t // 2, t % 2, :, :, :].rearrange("p t g d -> p (t g d)")))
                        m.then_inc(kst_ps, 1)
                    pe.wait_ge(qtokL, f + 1)
                    for a in range(PAIRS):
                        if a in (1, 2):
                            pe.wait_ge(kst_ok, 2 * f + a)
                        if a == 3:
                            pe.wait_ge(qst_ok, 4 * f + 1)
                        for j in range(GJ):
                            m = turn((W0, W1, W2, W0)[a][0:ROWS, j * P:(j + 1) * P],
                                     r32(Qtok[:, a * GJ + j, :, :].rearrange("p t d -> p (t d)")))
                        m.then_inc(qst_ps, 1)
                if back:
                    pe.wait_ge(on_ok, 4 * b + 4)
                    if front:
                        pe.wait_ge(qst_ok, 4 * f + 2)
                    for k in range(KB):
                        m = turn(W1[:, k * P:(k + 1) * P], on[:, k * 8:(k + 1) * 8, :].rearrange("p h d -> p (h d)"))
                    m.then_inc(aT_ps, 1)

                def scores(a):
                    pe.wait_ge(qst_ok, 4 * f + a + 1)
                    pe.wait_ge(kst_ok, 2 * f + a // 2 + 1)
                    if a < 2:
                        need(pe, exp_ok, 8 * f)
                    else:
                        pe.wait_ge(max_ok, 4 * f + a - 1)
                    for j in range(GJ):
                        m = pe.matmul(ps[:, 2 * (a % 2) + j // 2, (j % 2) * 2 * P:(j % 2 + 1) * 2 * P],
                                      Qst[0:ROWS, a, j * P:(j + 1) * P], Kst[0:ROWS, a, :, :], start=True, stop=True)
                    m.then_inc(s_ps, 1)
                if front:
                    scores(0)
                    scores(1)
                if back:
                    pe.wait_ge(aTL_ok, b + 1)
                    pe.wait_ge(woL_ok, 1)
                    if front:
                        pe.wait_ge(qst_ok, 4 * f + 3)
                    elif late:
                        pe.wait_ge(x2L_ok, i)
                    for k in range(KB):
                        c = slice(O0 + k * DM, O0 + (k + 1) * DM)
                        m = three(W2, aTH[:, k * P:(k + 1) * P], aTL[:, k * P:(k + 1) * P],
                                  WpH[:, c], WpL[:, c], k == 0, k == KB - 1)
                    m.then_inc(o_ps, 1)
                if front:
                    scores(2)
                    scores(3)

            pe.wait_ge(consts, 7)
            pe.wait_ge(selrows, 1)
            attention(pe, step)

            def gu(c, s, h):
                pe.wait_ge(w13L_ok, c + 1)
                need(pe, h_ok, c - 1)
                for m0, bank, done in ((0, (W0, W2)[s], g_ps), (KB, (W1, PVB)[s], u_ps)):
                    for k in range(KB):
                        w = slice((m0 + k) * P, (m0 + k + 1) * P)
                        t = slice(h * TOK, (h + 1) * TOK)
                        m = three(bank, w13H[:, s, w], w13L[:, s, w], x2H[:, k, t], x2L[:, k, t], k == 0, k == KB - 1)
                    m.then_inc(done, 1)

            def y(c, s, start, stop):
                pe.wait_ge(hL_ok, c + 1)
                pe.wait_ge(w2L_ok, c + 1)
                for t in range(HT):
                    w = slice(t * P, (t + 1) * P)
                    m = three(ps[:, t, :], hH[:, s, w], hL[:, s, w], w2H[:, s, :], w2L[:, s, :], start, stop)
                    if stop:
                        m.then_inc(y_ps, 1)
                if not stop:
                    m.then_inc(y_used, 1)

            pe.wait_ge(x2L_ok, NBATCH)
            for h in range(HALVES):
                c = h * NCH
                gu(c, 0, h)
                if h:
                    y(c - 1, 1, False, True)
                gu(c + 1, 1, h)
                if h:
                    pe.wait_ge(fin_ok, h * HT)
                y(c, 0, True, False)
                with pe.Fori(1, NCH // 2) as p:
                    gu(c + 2 * p, 0, h)
                    y(c + 2 * p - 1, 1, False, False)
                    gu(c + 2 * p + 1, 1, h)
                    y(c + 2 * p, 0, False, False)
            y(CHUNKS - 1, 1, False, True)


def kernel(**inputs):
    import numpy as np
    import concourse.bacc as bacc
    from concourse.bass_utils import run_bass_kernel_spmd

    f = {k: np.asarray(v) for k, v in inputs.items()}
    ctxt = f["ctx_4096"].reshape(NBATCH, P, KB, P).transpose(0, 3, 2, 1).reshape(NBATCH, P, DM)

    def rows(w):
        return w.reshape(KB, P, w.shape[1]).transpose(1, 0, 2).reshape(P, -1)

    def pairs(w):
        return w.reshape(-1, PAIRS, 2, GJ, DH).transpose(0, 1, 3, 2, 4).reshape(-1, DM)

    wkv = np.concatenate([f["L0_xattn_Wk"], f["L0_xattn_Wv"]], axis=1)
    wproj = np.concatenate([rows(wkv), rows(pairs(f["L0_xattn_Wq"])), rows(f["L0_xattn_Wo"])], axis=1)
    w1, w3 = (f[n].reshape(NCH, P, KB, P).transpose(0, 3, 2, 1).reshape(NCH, P, DM) for n in ("L0_ffn_w1", "L0_ffn_w3"))
    w2 = f["L0_ffn_w2"].reshape(DM, NCH, P).transpose(1, 2, 0)
    wff = np.concatenate([w1, w3, w2], axis=2)
    scales = np.concatenate([f["L0_ffn_w1_scale"], f["L0_ffn_w3_scale"], f["L0_ffn_w2_scale"].T], axis=1)
    small = np.concatenate([pairs(f["L0_xattn_bq"][None])[0], f["L0_xattn_bk"], f["L0_xattn_bv"], f["L0_xattn_bo"],
                            f["g_xattn"], f["g_ffn"], scales.reshape(-1)])[None]

    nc = bacc.Bacc("TRN2", target_bir_lowering=False, num_devices=1)
    arrays = {"x": f["x"], "ctxt": ctxt, "wproj": wproj, "small": small, "wff": wff}
    arrays = {k: np.ascontiguousarray(v) for k, v in arrays.items()}
    args = [nc.dram_tensor("in_" + k, v.shape, F32, kind="ExternalInput").ap() for k, v in arrays.items()]
    out = nc.dram_tensor("out", arrays["x"].shape, F32, kind="ExternalOutput").ap()
    build(nc, *args, out)
    r = run_bass_kernel_spmd(nc, [{"in_" + k: v for k, v in arrays.items()}], core_ids=[0])
    return r.results[0]["out"]
```

```python
from contextlib import ExitStack

import concourse.bass as bass
from concourse import mybir

F32 = mybir.dt.float32
F32R = mybir.dt.float32r
F16 = mybir.dt.float16
BF16 = mybir.dt.bfloat16
ALU = mybir.AluOpType
ACT = mybir.ActivationFunctionType
AX = mybir.AxisListType

P = 128
NBATCH = 8
DM = 512
KB = DM // P
HEADS = 32
KVH = 8
GJ = HEADS // KVH
DH = DM // HEADS
KVD = KVH * DH
PAIRS = KVH // 2
ROWS = 96
VC = 3 * DH + 1
FF = 1792
NCH = FF // P
HALVES = 2
HT = NBATCH // HALVES
TOK = HT * P
W13 = 2 * KB * P
CW = W13 + DM
NSC = CW // P
CHUNKS = HALVES * NCH
NEARLY = 3
NE, NL = 4, 4
EPS = 1e-5
SCALE = DH ** -0.5

KV0, Q0, O0 = 0, KB * 2 * KVD, KB * 2 * KVD + KB * DM
PW = O0 + KB * DM
BQ, BK, BO = 0, DM, DM + 2 * KVD
GATE, SC = BO + DM, BO + DM + 2
SMALL = SC + NCH * NSC


def build(nc, x, ctxt, wproj, small, wff, out):
    with ExitStack() as ctx:
        def sb(name, shape, dt=F32):
            return ctx.enter_context(nc.sbuf_tensor(name, shape, dt))

        def sem(name):
            return ctx.enter_context(nc.semaphore(name))

        def need(eng, s, n):
            if isinstance(n, int) and n <= 0:
                return
            eng.wait_ge(s, n)

        def r32(ap):
            return ap.bitcast(F32)

        X = sb("X", [P, NBATCH, DM])
        x2H = sb("x2H", [P, KB, NBATCH * P], F32R)
        x2L = sb("x2L", [P, KB, NBATCH * P], F32R)
        smallrow = sb("smallrow", [P, SMALL])
        tg = sb("tg", [P, 2])
        w13H = sb("w13H", [P, 2, W13], F32R)
        w13L = sb("w13L", [P, 2, W13], F32R)
        ps = ctx.enter_context(nc.psum_tensor("ps", [P, 8, 512], F32))
        W0, W1, W2, PVB = (ps[:, 4 + i, :] for i in range(4))

        att = ctx.enter_context(ExitStack())

        def sa(name, shape, dt=F32):
            return att.enter_context(nc.sbuf_tensor(name, shape, dt))

        raw = sa("raw", [P, PW])
        WpH = sa("WpH", [P, PW], F32R)
        WpL = sa("WpL", [P, PW], F32R)
        ident = sa("ident", [P, P])
        neghalf = sa("neghalf", [P, 1])
        sel = sa("sel", [P, 2, P])
        one2 = sa("one2", [P, P])
        ones = sa("ones", [P, P], F32R)
        brow = sa("brow", [P, GATE], F32R)
        ct = sa("ct", [P, DM])
        ctH = sa("ctH", [P, DM], F32R)
        ctL = sa("ctL", [P, DM], F32R)
        st1, mv1, ve1, rs1 = sa("st1", [P, 6]), sa("mv1", [P, 2]), sa("ve1", [P, 1]), sa("rs1", [P, 1])
        st2, mv2, ve2, rs2 = sa("st2", [P, 6]), sa("mv2", [P, 2]), sa("ve2", [P, 1]), sa("rs2", [P, 1])
        xn = sa("xn", [P, DM])
        xTH = sa("xTH", [P, DM], F32R)
        xTL = sa("xTL", [P, DM], F32R)
        Qtok = sa("Qtok", [P, PAIRS * GJ, 3, 32], F32R)
        Ktok = sa("Ktok", [P, PAIRS, 2, 3, 2, DH], F32R)
        Qst = sa("Qst", [P, PAIRS, GJ * P], F32R)
        Kst = sa("Kst", [P, PAIRS, 2, P], F32R)
        mx = sa("mx", [P, PAIRS, GJ, 2])
        Mtok = sa("Mtok", [P, PAIRS, GJ, 2, 2])
        vres = sa("vres", [P, KVH, DH])
        Vp = sa("Vp", [P, NBATCH, KVH, VC + 1], BF16)
        E = sa("E", [P, NE, GJ * P])
        PH = sa("PH", [P, KVH, GJ * P], F16)
        PL = sa("PL", [P, NL, GJ * P], F16)
        rden = sa("rden", [P, HEADS])
        on = sa("on", [P, HEADS, DH])
        aTH = sa("aTH", [P, DM], F32R)
        aTL = sa("aTL", [P, DM], F32R)
        x2n = sa("x2n", [P, DM])
        att.close()

        wres = sb("wres", [P, NCH, CW])
        w2H = sb("w2H", [P, 2, DM], F32R)
        w2L = sb("w2L", [P, 2, DM], F32R)
        T = sb("T", [P, 2, TOK])
        A = sb("A", [P, 2, TOK])
        hf = sb("hf", [P, 2, TOK])
        hH = sb("hH", [P, 2, TOK], F32R)
        hL = sb("hL", [P, 2, TOK], F32R)

        small_in, wkv_in, wq_in, wo_in = sem("small_in"), sem("wkv_in"), sem("wq_in"), sem("wo_in")
        x_in, xres_in, ct_in = sem("x_in"), sem("xres_in"), sem("ct_in")
        wff_in = [sem(f"wff_in{c}") for c in range(NCH)]
        consts = sem("consts")
        zeros = sem("zeros")
        selrows = sem("selrows")
        tanhg = sem("tanhg")
        browH_ok, brow_ok = sem("browH_ok"), sem("brow_ok")
        wpH_ok, wpL_ok, woL_ok = sem("wpH_ok"), sem("wpL_ok"), sem("woL_ok")
        stats1, mean1, ve1_ok, rs1_ok, xn_ok = (sem(n) for n in ("stats1", "mean1", "ve1_ok", "rs1_ok", "xn_ok"))
        stats2, mean2, ve2_ok, rs2_ok, x2n_ok = (sem(n) for n in ("stats2", "mean2", "ve2_ok", "rs2_ok", "x2n_ok"))
        ctH_ok, ctL_ok = sem("ctH_ok"), sem("ctL_ok")
        xT_ps, xTH_ok, xTL_ok = sem("xT_ps"), sem("xTH_ok"), sem("xTL_ok")
        kv_ps, q_ps = sem("kv_ps"), sem("q_ps")
        qtokH, qtokL, ktokH, ktokL = sem("qtokH"), sem("qtokL"), sem("ktokH"), sem("ktokL")
        v1_ok, r1_ok, v2_ok, v3_ok = sem("v1_ok"), sem("r1_ok"), sem("v2_ok"), sem("v3_ok")
        kst_ps, kst_ok, qst_ps, qst_ok = sem("kst_ps"), sem("kst_ok"), sem("qst_ps"), sem("qst_ok")
        s_ps, max_ok, mH_ok, mL_ok = sem("s_ps"), sem("max_ok"), sem("mH_ok"), sem("mL_ok")
        mT_ps, mrows = sem("mT_ps"), sem("mrows")
        st_ps, exp_ok, pL_ok = sem("st_ps"), sem("exp_ok"), sem("pL_ok")
        pv_ps, pv_read, on_ok = sem("pv_ps"), sem("pv_read"), sem("on_ok")
        aT_ps, aTH_ok, aTL_ok = sem("aT_ps"), sem("aTH_ok"), sem("aTL_ok")
        o_ps, x2_ok, xcopy_ok = sem("o_ps"), sem("x2_ok"), sem("xcopy_ok")
        x2T_ps, x2H_ok, x2L_ok = sem("x2T_ps"), sem("x2H_ok"), sem("x2L_ok")
        scaled = sem("scaled")
        w13H_ok, w13L_ok, w2H_ok, w2L_ok = sem("w13H_ok"), sem("w13L_ok"), sem("w2H_ok"), sem("w2L_ok")
        g_ps, u_ps, t_ok, a_ok, h_ok, hH_ok, hL_ok = (sem(n) for n in ("g_ps", "u_ps", "t_ok", "a_ok", "h_ok", "hH_ok", "hL_ok"))
        y_used = sem("y_used")
        y_ps, fin_ok, out_done = sem("y_ps"), sem("fin_ok"), sem("out_done")

        block = ctx.enter_context(nc.Block())

        def first(i):
            return isinstance(i, int) and i == -2

        def attention(eng, step):
            for i in (-2, -1, 0):
                step(i, i + 2, i + 1 if i > -2 else None, i if i > -1 else None, None)
            with eng.Fori(1, NBATCH - 2) as i:
                step(i, i + 2, i + 1, i, i - 1)
            for i in (NBATCH - 2, NBATCH - 1, NBATCH):
                step(i, None, i + 1 if i < NBATCH - 1 else None, i if i < NBATCH else None, i - 1)

        def feed_forward(eng, ffn):
            for h in range(HALVES):
                c0 = h * NCH
                ffn(h, c0, 0, 0, 1)
                ffn(h, c0 + 1, 1, 1, 2)
                with eng.Fori(1, NCH // 2 - 1) as p:
                    ffn(h, c0 + 2 * p, 2 * p, 0, 2 * p + 1)
                    ffn(h, c0 + 2 * p + 1, 2 * p + 1, 1, 2 * p + 2)
                ffn(h, c0 + NCH - 2, NCH - 2, 0, NCH - 1)
                ffn(h, c0 + NCH - 1, NCH - 1, 1, 0 if h < HALVES - 1 else None)

        @block.sync
        def _(sp):
            sp.dma_start(xn[:], x[0]).then_inc(x_in, 16)
            sp.dma_start(smallrow[:], small.broadcast_to([P, SMALL])).then_inc(small_in, 16)
            sp.dma_start(raw[:, Q0:O0], wproj[:, Q0:O0]).then_inc(wq_in, 16)
            sp.dma_start(raw[:, O0:PW], wproj[:, O0:PW]).then_inc(wo_in, 16)
            sp.wait_ge(xT_ps, 1)
            sp.dma_start(xn[:], x[1]).then_inc(x_in, 16)
            sp.wait_ge(ctL_ok, 1)
            sp.dma_start(ct[:], ctxt[1]).then_inc(ct_in, 16)
            sp.dma_start(X[:], x.rearrange("b p n -> p b n")).then_inc(xres_in, 16)
            with sp.Fori(2, NBATCH) as b:
                sp.wait_ge(ctL_ok, b)
                sp.dma_start(ct[:], ctxt[b]).then_inc(ct_in, 16)
                sp.wait_ge(xT_ps, b)
                sp.dma_start(xn[:], x[b]).then_inc(x_in, 16)
            sp.wait_ge(wpL_ok, 2)
            sp.wait_ge(woL_ok, 1)
            for c in range(NCH):
                if c == NEARLY:
                    sp.wait_ge(x2L_ok, NBATCH)
                sp.dma_start(wres[:, c, :], wff[c]).then_inc(wff_in[c], 16)
            with sp.Fori(0, NBATCH) as t:
                sp.wait_ge(fin_ok, t + 1)
                sp.dma_start(out[t], X[:, t, :]).then_inc(out_done, 16)
            sp.wait_ge(out_done, 16 * NBATCH)

        @block.gpsimd
        def _(pool):
            pool.memset(neghalf[:], -0.5).then_inc(consts, 1)
            pool.memset(ident[:], 0.0).then_inc(consts, 1)
            pool.memset(one2[:], 0.0).then_inc(consts, 1)
            pool.memset(sel[:], 1.0).then_inc(consts, 1)
            pool.wait_ge(consts, 4)
            pool.affine_select(out=ident[:], in_=ident[:], compare_op=ALU.not_equal, fill=1.0, base=0,
                               pattern=[[-1, P]], channel_multiplier=1).then_inc(consts, 1)
            pool.affine_select(out=one2[:], in_=one2[:], compare_op=ALU.not_equal, fill=1.0, base=0,
                               pattern=[[0, P]], channel_multiplier=1).then_inc(consts, 1)
            pool.affine_select(out=sel[:], in_=sel[:], compare_op=ALU.is_ge, fill=0.0, base=-ROWS,
                               pattern=[[-2, 2], [0, P]], channel_multiplier=1).then_inc(consts, 1)
            pool.wait_ge(consts, 7)
            pool.affine_select(out=one2[:], in_=one2[:], compare_op=ALU.not_equal, fill=1.0, base=-32,
                               pattern=[[0, P]], channel_multiplier=1).then_inc(consts, 1)
            pool.affine_select(out=sel[:], in_=sel[:], compare_op=ALU.is_ge, fill=0.0, base=ROWS + 1,
                               pattern=[[2, 2], [0, P]], channel_multiplier=-1).then_inc(consts, 1)

            def step(i, a, f, b, l):
                if a is not None:
                    pool.wait_ge(ctH_ok, a + 1)
                    need(pool, kv_ps, a)
                    pool.tensor_tensor(ctL[:], ct[:], r32(ctH[:]), ALU.subtract).then_inc(ctL_ok, 1)
                    need(pool, xn_ok, a)
                    pool.wait_ge(ve1_ok, a + 1)
                    pool.tensor_tensor(rs1[:], ve1[:], neghalf[:], ALU.pow).then_inc(rs1_ok, 1)
                if first(i):
                    pool.memset(Vp[:, :, :, 3 * DH:VC], 1.0).then_inc(consts, 1)
                    pool.wait_ge(wpH_ok, 3)
                    pool.tensor_tensor(WpL[:, O0:PW], raw[:, O0:PW], r32(WpH[:, O0:PW]), ALU.subtract).then_inc(woL_ok, 1)

                def low(g):
                    pool.wait_ge(exp_ok, 2 * (8 * b + g + 1))
                    need(pool, pv_ps, 8 * b + g - NL + 1)
                    pool.tensor_tensor(PL[:, g % NL, :], E[:, g % NE, :], PH[:, g, :], ALU.subtract).then_inc(pL_ok, 1)
                if b is not None:
                    for g in range(3):
                        low(g)
                if l is not None:
                    need(pool, x2n_ok, l)
                    pool.wait_ge(ve2_ok, l + 1)
                    pool.tensor_tensor(rs2[:], ve2[:], neghalf[:], ALU.pow).then_inc(rs2_ok, 1)
                if b is not None:
                    for g in range(3, KVH):
                        low(g)

            attention(pool, step)

            for c in range(NCH):
                w = wres[:, c, :].rearrange("p (a n) -> p a n", n=P)
                s = smallrow[:, SC + c * NSC:SC + (c + 1) * NSC].unsqueeze(2).broadcast_to([P, NSC, P])
                pool.wait_ge(wff_in[c], 16)
                pool.tensor_tensor(w, w, s, ALU.mult).then_inc(scaled, 1)

        @block.scalar
        def _(act):
            act.dma_start(ct[:], ctxt[0]).then_inc(ct_in, 16)
            act.dma_start(raw[:, KV0:Q0], wproj[:, KV0:Q0]).then_inc(wkv_in, 16)

            def weights_high(s, c0, c1):
                act.wait_ge(s, 16)
                act.activation(WpH[:, c0:c1], raw[:, c0:c1], ACT.Copy).then_inc(wpH_ok, 1)

            def step(i, a, f, b, l):
                if a is not None:
                    act.wait_ge(ct_in, 16 * (a + 1))
                    need(act, kv_ps, a)
                    act.activation(ctH[:], ct[:], ACT.Copy).then_inc(ctH_ok, 1)
                if first(i):
                    weights_high(wkv_in, KV0, Q0)
                    act.wait_ge(small_in, 16)
                    act.activation(tg[:], smallrow[:, GATE:GATE + 2], ACT.Tanh).then_inc(tanhg, 1)
                    act.activation(brow[:], smallrow[:, 0:GATE], ACT.Copy).then_inc(browH_ok, 1)
                    weights_high(wq_in, Q0, O0)

                def exps(g):
                    act.wait_ge(st_ps, 8 * b + g + 1)
                    need(act, pL_ok, 8 * b + g - NE + 1)
                    act.activation(E[:, g % NE, :], ps[:, g % 4, :], ACT.Exp, scale=SCALE).then_inc(exp_ok, 1)
                    need(act, pv_ps, 8 * b + g - KVH + 1)
                    act.activation(PH[:, g, :], ps[:, g % 4, :], ACT.Exp, scale=SCALE).then_inc(exp_ok, 1)
                if b is not None:
                    exps(0)
                    exps(1)
                if l is not None:
                    act.wait_ge(aT_ps, l + 1)
                    need(act, o_ps, l)
                    act.activation(aTH[:], W0, ACT.Copy).then_inc(aTH_ok, 1)
                if b is not None:
                    for g in range(2, 6):
                        exps(g)
                if a is not None:
                    act.wait_ge(xT_ps, a + 1)
                    need(act, q_ps, a)
                    act.activation(xTH[:], W0, ACT.Copy).then_inc(xTH_ok, 1)
                if b is not None:
                    exps(6)
                    exps(7)
                if f is not None:
                    need(act, st_ps, 8 * f)
                    for h in range(2):
                        act.wait_ge(kst_ps, 2 * f + h + 1)
                        act.activation(Kst[0:ROWS, 2 * h:2 * h + 2, :, :],
                                       (W1, W2)[h][0:ROWS, :].rearrange("p (a g k) -> p a g k", a=2, g=2),
                                       ACT.Copy).then_inc(kst_ok, 1)
                    for h in range(PAIRS):
                        act.wait_ge(qst_ps, 4 * f + h + 1)
                        act.activation(Qst[0:ROWS, h, :], (W0, W1, W2, W1)[h][0:ROWS, :], ACT.Copy).then_inc(qst_ok, 1)
                if a is not None:
                    act.wait_ge(kv_ps, a + 1)
                    need(act, ktokL, 2 * a)
                    for gg in range(2):
                        act.activation(Ktok[:, :, gg, 0:2, gg, :],
                                       W0[:, 0:KVD].rearrange("p (a g d) -> p a g d", a=PAIRS, g=2)[:, :, gg, :]
                                       .unsqueeze(2).broadcast_to([P, PAIRS, 2, DH]), ACT.Copy).then_inc(ktokH, 1)
                    act.wait_ge(q_ps, a + 1)
                    need(act, qst_ps, 4 * a)
                    need(act, qtokL, a)
                    act.activation(Qtok[:, :, 0:3:2, :], W1.rearrange("p (a d) -> p a d", d=32)
                                   .unsqueeze(2).broadcast_to([P, PAIRS * GJ, 2, 32]), ACT.Copy).then_inc(qtokH, 1)
                if l is not None:
                    act.wait_ge(x2T_ps, l + 1)
                    act.activation(x2H[:, :, bass.ds(l * P, P)], W2.rearrange("p (k n) -> p k n", k=KB),
                                   ACT.Copy).then_inc(x2H_ok, 1)
                if f is not None:
                    for h in range(PAIRS):
                        act.wait_ge(mT_ps, 4 * f + h + 1)
                        act.activation(Qst[ROWS:ROWS + 4, h, :], (W0, W1, W2, W0)[h][0:4, :], ACT.Copy).then_inc(mrows, 1)
                if first(i):
                    weights_high(wo_in, O0, PW)

            attention(act, step)

            def ffn(h, c, n, s, ahead):
                if ahead is not None:
                    split13(c + 1, ahead, 1 - s)
                act.wait_ge(g_ps, c + 1)
                need(act, a_ok, c - 1)
                act.activation(T[:, s, :], (W0, W2)[s], ACT.Tanh, scale=0.5).then_inc(t_ok, 1)
                need(act, y_used, c - 1 - h)
                act.activation(w2H[:, s, :], wres[:, n, W13:CW], ACT.Copy).then_inc(w2H_ok, 1)
                act.wait_ge(h_ok, c + 1)
                act.activation(hH[:, s, :], hf[:, s, :], ACT.Copy).then_inc(hH_ok, 1)

            def split13(c, n, s):
                act.wait_ge(scaled, n + 1)
                need(act, u_ps, c - 1)
                act.activation(w13H[:, s, :], wres[:, n, 0:W13], ACT.Copy).then_inc(w13H_ok, 1)

            split13(0, 0, 0)
            feed_forward(act, ffn)

        @block.vector
        def _(dve):
            dve.memset(r32(Ktok[:]), 0.0).then_inc(zeros, 1)
            dve.memset(r32(Qst[ROWS:P, :, :]), 0.0).then_inc(zeros, 1)

            def weights_low(n, c0, c1):
                dve.wait_ge(wpH_ok, n)
                dve.tensor_tensor(WpL[:, c0:c1], raw[:, c0:c1], r32(WpH[:, c0:c1]), ALU.subtract).then_inc(wpL_ok, 1)

            def step(i, a, f, b, l):
                if a is not None:
                    dve.wait_ge(x_in, 16 * (a + 1))
                    dve.bn_stats(st1[:], xn[:]).then_inc(stats1, 1)
                    dve.wait_ge(stats1, a + 1)
                if l is not None:
                    dve.wait_ge(aTH_ok, l + 1)
                    dve.tensor_tensor(aTL[:], W0, r32(aTH[:]), ALU.subtract).then_inc(aTL_ok, 1)
                if a is not None:
                    dve.bn_aggr(mv1[:], st1[:]).then_inc(mean1, 1)
                    dve.wait_ge(mean1, a + 1)
                    dve.tensor_scalar(ve1[:], mv1[:, 1:2], EPS, None, ALU.add).then_inc(ve1_ok, 1)
                if first(i):
                    dve.wait_ge(consts, 9)
                    dve.tensor_copy(ones[:], one2[:]).then_inc(selrows, 1)
                    dve.wait_ge(browH_ok, 1)
                    dve.tensor_tensor(brow[32:64, :], smallrow[32:64, 0:GATE], r32(brow[32:64, :]),
                                      ALU.subtract).then_inc(brow_ok, 1)
                    weights_low(1, KV0, Q0)
                if a is not None:
                    dve.wait_ge(rs1_ok, a + 1)
                    dve.tensor_scalar(xn[:], xn[:], mv1[:, 0:1], rs1[:, 0:1], ALU.subtract, ALU.mult).then_inc(xn_ok, 1)
                if first(i):
                    dve.tensor_copy(Kst[ROWS:P, :, :, :], sel[ROWS:P, :, :].unsqueeze(1)
                                    .broadcast_to([P - ROWS, PAIRS, 2, P])).then_inc(selrows, 1)
                    weights_low(2, Q0, O0)
                if l is not None:
                    dve.wait_ge(o_ps, l + 1)
                    if isinstance(l, int) and l == 0:
                        dve.wait_ge(xres_in, 16)
                    need(dve, x2T_ps, l)
                    dve.scalar_tensor_tensor(out=x2n[:], in0=W2, scalar=tg[:, 0:1], in1=X[:, l, :],
                                             op0=ALU.mult, op1=ALU.add).then_inc(x2_ok, 1)
                if l is not None:
                    dve.wait_ge(x2_ok, l + 1)
                    dve.bn_stats(st2[:], x2n[:]).then_inc(stats2, 1)
                    dve.tensor_copy(X[:, l, :], x2n[:]).then_inc(xcopy_ok, 1)
                    dve.wait_ge(stats2, l + 1)
                if a is not None:
                    dve.wait_ge(xTH_ok, a + 1)
                    dve.tensor_tensor(xTL[:], W0, r32(xTH[:]), ALU.subtract).then_inc(xTL_ok, 1)
                if l is not None:
                    dve.bn_aggr(mv2[:], st2[:]).then_inc(mean2, 1)
                    dve.wait_ge(mean2, l + 1)
                    dve.tensor_scalar(ve2[:], mv2[:, 1:2], EPS, None, ALU.add).then_inc(ve2_ok, 1)

                def pv_sum(q):
                    n = 4 * b + q
                    dve.wait_ge(pv_ps, 8 * b + 2 * q + 2)
                    if q == 0:
                        need(dve, aT_ps, b)
                    v = PVB[:, 0:8 * VC].rearrange("p (h c) -> p h c", c=VC)
                    o = on[:, 8 * q:8 * q + 8, :]
                    r = rden[:, 8 * q:8 * q + 8]
                    dve.tensor_reduce(o, v[:, :, 0:3 * DH].rearrange("p h (t d) -> p h d t", t=3), AX.X, ALU.add).then_inc(pv_read, 1)
                    dve.reciprocal(r, v[:, :, 3 * DH]).then_inc(pv_read, 1)
                    dve.wait_ge(pv_read, 2 * n + 2)
                    dve.tensor_tensor(o, o, r.unsqueeze(2).broadcast_to([P, 8, DH]), ALU.mult).then_inc(on_ok, 1)

                def maxima(h):
                    dve.wait_ge(s_ps, 4 * f + h + 1)
                    dve.tensor_reduce(mx[:, h, :, :],
                                      ps[:, 2 * (h % 2):2 * (h % 2) + 2, :].rearrange("p b (j g k) -> p (b j) g k", j=2, g=2),
                                      AX.X, ALU.max).then_inc(max_ok, 1)
                    dve.wait_ge(max_ok, 4 * f + h + 1)
                    need(dve, mT_ps, 4 * (f - 1) + h + 1)
                    dve.tensor_scalar(Mtok[:, h, :, :, 0].bitcast(F32R), mx[:, h, :, :], -1.0, None, ALU.mult).then_inc(mH_ok, 1)
                    dve.wait_ge(mH_ok, 4 * f + h + 1)
                    dve.scalar_tensor_tensor(out=Mtok[:, h, :, :, 1], in0=mx[:, h, :, :], scalar=-1.0,
                                             in1=Mtok[:, h, :, :, 0], op0=ALU.mult, op1=ALU.subtract).then_inc(mL_ok, 1)

                if l is not None:
                    dve.wait_ge(rs2_ok, l + 1)
                    dve.wait_ge(xcopy_ok, l + 1)
                    dve.tensor_scalar(x2n[:], x2n[:], mv2[:, 0:1], rs2[:, 0:1], ALU.subtract, ALU.mult).then_inc(x2n_ok, 1)
                if b is not None:
                    pv_sum(0)
                if b is not None:
                    pv_sum(1)
                if a is not None:
                    dve.wait_ge(ktokH, 2 * a + 2)
                    for gg in range(2):
                        dve.tensor_tensor(Ktok[:, :, gg, 2, gg, :],
                                          W0[:, 0:KVD].rearrange("p (a g d) -> p a g d", a=PAIRS, g=2)[:, :, gg, :],
                                          r32(Ktok[:, :, gg, 0, gg, :]), ALU.subtract).then_inc(ktokL, 1)
                    v = W0[:, KVD:2 * KVD].rearrange("p (g d) -> p g d", g=KVH)
                    vp = Vp[:, a, :, :]
                    dve.tensor_copy(vp[:, :, 0:DH], v).then_inc(v1_ok, 1)
                    dve.wait_ge(v1_ok, a + 1)
                    dve.tensor_tensor(vres[:], v, vp[:, :, 0:DH], ALU.subtract).then_inc(r1_ok, 1)
                    dve.wait_ge(r1_ok, a + 1)
                    dve.tensor_copy(vp[:, :, DH:2 * DH], vres[:]).then_inc(v2_ok, 1)
                    dve.wait_ge(v2_ok, a + 1)
                    dve.tensor_tensor(vp[:, :, 2 * DH:3 * DH], vres[:], vp[:, :, DH:2 * DH], ALU.subtract).then_inc(v3_ok, 1)
                    dve.wait_ge(qtokH, a + 1)
                    dve.tensor_tensor(Qtok[:, :, 1, :], W1.rearrange("p (a d) -> p a d", d=32),
                                      r32(Qtok[:, :, 0, :]), ALU.subtract).then_inc(qtokL, 1)
                if f is not None:
                    maxima(0)
                    maxima(1)
                if l is not None:
                    dve.wait_ge(x2H_ok, l + 1)
                    dve.tensor_tensor(x2L[:, :, bass.ds(l * P, P)], W2.rearrange("p (k n) -> p k n", k=KB),
                                      r32(x2H[:, :, bass.ds(l * P, P)]), ALU.subtract).then_inc(x2L_ok, 1)
                if b is not None:
                    pv_sum(2)
                if f is not None:
                    maxima(2)
                    maxima(3)
                if b is not None:
                    pv_sum(3)

            attention(dve, step)

            def split13(c, n, s):
                dve.wait_ge(w13H_ok, c + 1)
                dve.tensor_tensor(w13L[:, s, :], wres[:, n, 0:W13], r32(w13H[:, s, :]), ALU.subtract).then_inc(w13L_ok, 1)

            def final(h):
                for t in range(HT):
                    n = h * HT + t
                    dve.wait_ge(y_ps, n + 1)
                    dve.scalar_tensor_tensor(out=X[:, n, :], in0=ps[:, t, :], scalar=tg[:, 1:2], in1=X[:, n, :],
                                             op0=ALU.mult, op1=ALU.add).then_inc(fin_ok, 1)

            def ffn(h, c, n, s, ahead):
                if ahead is not None:
                    split13(c + 1, ahead, 1 - s)
                if isinstance(c, int) and c == NCH:
                    final(0)
                dve.wait_ge(t_ok, c + 1)
                need(dve, h_ok, c - 1)
                dve.scalar_tensor_tensor(out=A[:, s, :], in0=T[:, s, :], scalar=1.0, in1=(W0, W2)[s],
                                         op0=ALU.add, op1=ALU.mult).then_inc(a_ok, 1)
                dve.wait_ge(u_ps, c + 1)
                dve.wait_ge(a_ok, c + 1)
                need(dve, hL_ok, c - 1)
                dve.scalar_tensor_tensor(out=hf[:, s, :], in0=A[:, s, :], scalar=0.5, in1=(W1, PVB)[s],
                                         op0=ALU.mult, op1=ALU.mult).then_inc(h_ok, 1)
                dve.wait_ge(w2H_ok, c + 1)
                dve.tensor_tensor(w2L[:, s, :], wres[:, n, W13:CW], r32(w2H[:, s, :]), ALU.subtract).then_inc(w2L_ok, 1)
                dve.wait_ge(hH_ok, c + 1)
                dve.tensor_tensor(hL[:, s, :], hf[:, s, :], r32(hH[:, s, :]), ALU.subtract).then_inc(hL_ok, 1)

            split13(0, 0, 0)
            feed_forward(dve, ffn)
            final(1)

        @block.tensor
        def _(pe):
            def three(out_ap, aH, aL, bH, bL, start, stop):
                pe.matmul(out_ap, aH, bH, start=start, stop=False)
                pe.matmul(out_ap, aH, bL, start=False, stop=False)
                return pe.matmul(out_ap, aL, bH, start=False, stop=stop)

            def turn(out_ap, in_ap):
                return pe.matmul(out_ap, in_ap, ident[:], start=True, stop=True, is_transpose=True)

            def project(bank, width, H, L, w0, bias):
                pe.matmul(bank[:, 0:width], ones[:], brow[:, bias:bias + width], start=True, stop=False)
                for k in range(KB):
                    c = slice(w0 + k * width, w0 + (k + 1) * width)
                    m = three(bank[:, 0:width], H[:, k * P:(k + 1) * P], L[:, k * P:(k + 1) * P],
                              WpH[:, c], WpL[:, c], False, k == KB - 1)
                return m

            def step(i, a, f, b, l):
                def scores_t(g):
                    pe.wait_ge(mrows, 4 * b + g // 2 + 1)
                    if g == 0:
                        pe.wait_ge(max_ok, 4 * b + 3)
                    if g == 2:
                        pe.wait_ge(max_ok, 4 * b + 4)
                    if g >= 4:
                        pe.wait_ge(exp_ok, 2 * (8 * b + g - 3))
                    pe.matmul(ps[:, g % 4, :], Kst[:, g // 2, g % 2, :], Qst[:, g // 2, :],
                              start=True, stop=True).then_inc(st_ps, 1)

                def values(g):
                    pe.wait_ge(pL_ok, 8 * b + g + 1)
                    if g % 2 == 0:
                        need(pe, pv_read, 2 * (4 * b + g // 2))
                    for j in range(GJ):
                        h = (g % 2) * GJ + j
                        o = PVB[:, h * VC:(h + 1) * VC]
                        v = Vp[:, b, g, 0:VC]
                        pe.matmul(o, PH[:, g, j * P:(j + 1) * P], v, start=True, stop=False)
                        m = pe.matmul(o, PL[:, g % NL, j * P:(j + 1) * P], v, start=False, stop=True)
                    m.then_inc(pv_ps, 1)

                def stack_q(h):
                    if h == 0 and a is not None:
                        pe.wait_ge(xTL_ok, a + 1)
                    if h in (1, 2):
                        pe.wait_ge(kst_ok, 2 * f + h)
                    if h == 3:
                        pe.wait_ge(qst_ok, 4 * f + 2)
                    for j in range(GJ):
                        m = turn((W0, W1, W2, W1)[h][0:ROWS, j * P:(j + 1) * P],
                                 r32(Qtok[:, h * GJ + j, :, :].rearrange("p t d -> p (t d)")))
                    m.then_inc(qst_ps, 1)

                def scores(h):
                    pe.wait_ge(qst_ok, 4 * f + h + 1)
                    if h < 2:
                        if b is not None:
                            pe.wait_ge(exp_ok, 2 * (8 * b + 6 + 2 * h))
                    else:
                        pe.wait_ge(max_ok, 4 * f + h - 1)
                    for j in range(GJ):
                        m = pe.matmul(ps[:, 2 * (h % 2) + j // 2, (j % 2) * 2 * P:(j % 2 + 1) * 2 * P],
                                      Qst[0:ROWS, h, j * P:(j + 1) * P], Kst[0:ROWS, h, :, :], start=True, stop=True)
                    m.then_inc(s_ps, 1)

                def rows_max(h):
                    pe.wait_ge(mL_ok, 4 * f + h + 1)
                    if h == 0 and a is None:
                        pe.wait_ge(qst_ok, 4 * f + 1)
                    if h == 0 and a is not None:
                        pe.wait_ge(r1_ok, a + 1)
                    if h == 1 and a is None:
                        pe.wait_ge(qst_ok, 4 * f + 4)
                    if h == 1 and a is not None:
                        pe.wait_ge(qtokL, a + 1)
                    if h == 2 and l is not None:
                        pe.wait_ge(x2L_ok, l + 1)
                    if h == 3:
                        pe.wait_ge(mrows, 4 * f + 1)
                    for j in range(GJ):
                        m = turn((W0, W1, W2, W0)[h][0:4, j * P:(j + 1) * P],
                                 Mtok[:, h, j, :, :].rearrange("p g t -> p (g t)"))
                    m.then_inc(mT_ps, 1)

                if b is not None:
                    for g in range(4):
                        scores_t(g)
                if l is not None:
                    pe.wait_ge(on_ok, 4 * l + 4)
                    pe.wait_ge(mrows, min(4 * (l + 2), 4 * NBATCH) if isinstance(l, int) else 4 * (l + 2))
                    for k in range(KB):
                        m = turn(W0[:, k * P:(k + 1) * P], on[:, k * 8:(k + 1) * 8, :].rearrange("p h d -> p (h d)"))
                    m.then_inc(aT_ps, 1)
                if b is not None:
                    scores_t(4)
                    scores_t(5)
                if l is not None:
                    pe.wait_ge(aTL_ok, l + 1)
                    pe.wait_ge(woL_ok, 1)
                    need(pe, x2L_ok, l)
                    project(W2, DM, aTH, aTL, O0, BO).then_inc(o_ps, 1)
                if b is not None:
                    scores_t(6)
                    scores_t(7)
                if a is not None:
                    pe.wait_ge(xn_ok, a + 1)
                    if f is not None:
                        need(pe, mrows, 4 * f)
                    for k in range(KB):
                        m = turn(W0[:, k * P:(k + 1) * P], xn[:, k * P:(k + 1) * P])
                    m.then_inc(xT_ps, 1)
                if b is not None:
                    pe.wait_ge(v3_ok, b + 1)
                    values(0)
                    values(1)
                if f is not None:
                    pe.wait_ge(ktokL, 2 * f + 2)
                    pe.wait_ge(qtokL, f + 1)
                    for h in range(2):
                        if h == 0 and isinstance(i, int) and i == -1:
                            pe.wait_ge(qtokL, 1)
                        elif h == 0:
                            pe.wait_ge(mrows, 4 * f)
                        if h == 1 and l is not None:
                            pe.wait_ge(x2_ok, l + 1)
                        for t in range(4):
                            m = turn((W1, W2)[h][0:ROWS, t * P:(t + 1) * P],
                                     r32(Ktok[:, 2 * h + t // 2, t % 2, :, :, :].rearrange("p t g d -> p (t g d)")))
                        m.then_inc(kst_ps, 1)
                    stack_q(0)
                    stack_q(1)
                if b is not None:
                    values(2)
                if f is not None:
                    stack_q(2)
                    stack_q(3)
                if b is not None:
                    values(3)
                if a is not None:
                    pe.wait_ge(ctL_ok, a + 1)
                    if first(i):
                        pe.wait_ge(selrows, 1)
                        pe.wait_ge(brow_ok, 1)
                        pe.wait_ge(wpL_ok, 1)
                    pe.wait_ge(xTL_ok, a + 1)
                    if f is not None:
                        pe.wait_ge(qst_ok, 4 * f + 1)
                    project(W0, 2 * KVD, ctH, ctL, KV0, BK).then_inc(kv_ps, 1)
                    if first(i):
                        pe.wait_ge(wpL_ok, 2)
                    if f is not None:
                        pe.wait_ge(qst_ok, 4 * f + 4)
                    project(W1, DM, xTH, xTL, Q0, BQ).then_inc(q_ps, 1)
                if f is not None:
                    scores(0)
                    scores(1)
                if b is not None:
                    values(4)
                if l is not None:
                    pe.wait_ge(x2n_ok, l + 1)
                    if f is not None:
                        pe.wait_ge(qst_ok, 4 * f + 3)
                    for k in range(KB):
                        m = turn(W2[:, k * P:(k + 1) * P], x2n[:, k * P:(k + 1) * P])
                    m.then_inc(x2T_ps, 1)
                if b is not None:
                    values(5)
                if f is not None:
                    rows_max(0)
                    scores(2)
                    rows_max(1)
                    scores(3)
                if b is not None:
                    values(6)
                    values(7)
                if f is not None:
                    rows_max(2)
                    rows_max(3)

            pe.wait_ge(consts, 9)
            pe.wait_ge(zeros, 2)
            attention(pe, step)

            def gu(c, s, h):
                pe.wait_ge(w13L_ok, c + 1)
                need(pe, h_ok, c - 1)
                for m0, bank, done in ((0, (W0, W2)[s], g_ps), (KB, (W1, PVB)[s], u_ps)):
                    for k in range(KB):
                        w = slice((m0 + k) * P, (m0 + k + 1) * P)
                        t = slice(h * TOK, (h + 1) * TOK)
                        m = three(bank, w13H[:, s, w], w13L[:, s, w], x2H[:, k, t], x2L[:, k, t], k == 0, k == KB - 1)
                    m.then_inc(done, 1)

            def y(c, s, start, stop):
                pe.wait_ge(hL_ok, c + 1)
                pe.wait_ge(w2L_ok, c + 1)
                for t in range(HT):
                    w = slice(t * P, (t + 1) * P)
                    m = three(ps[:, t, :], hH[:, s, w], hL[:, s, w], w2H[:, s, :], w2L[:, s, :], start, stop)
                    if stop:
                        m.then_inc(y_ps, 1)
                if not stop:
                    m.then_inc(y_used, 1)

            pe.wait_ge(x2L_ok, NBATCH)
            for h in range(HALVES):
                c = h * NCH
                gu(c, 0, h)
                if h:
                    y(c - 1, 1, False, True)
                gu(c + 1, 1, h)
                if h:
                    pe.wait_ge(fin_ok, h * HT)
                y(c, 0, True, False)
                with pe.Fori(1, NCH // 2) as p:
                    gu(c + 2 * p, 0, h)
                    y(c + 2 * p - 1, 1, False, False)
                    gu(c + 2 * p + 1, 1, h)
                    y(c + 2 * p, 0, False, False)
            y(CHUNKS - 1, 1, False, True)


def kernel(**inputs):
    import numpy as np
    import concourse.bacc as bacc
    from concourse.bass_utils import run_bass_kernel_spmd

    f = {k: np.asarray(v) for k, v in inputs.items()}
    ctxt = f["ctx_4096"].reshape(NBATCH, P, KB, P).transpose(0, 3, 2, 1).reshape(NBATCH, P, DM)

    def rows(w):
        return w.reshape(KB, P, w.shape[1]).transpose(1, 0, 2).reshape(P, -1)

    def pairs(w):
        return w.reshape(-1, PAIRS, 2, GJ, DH).transpose(0, 1, 3, 2, 4).reshape(-1, DM)

    wkv = np.concatenate([f["L0_xattn_Wk"], f["L0_xattn_Wv"]], axis=1)
    wproj = np.concatenate([rows(wkv), rows(pairs(f["L0_xattn_Wq"])), rows(f["L0_xattn_Wo"])], axis=1)
    w1, w3 = (f[n].reshape(NCH, P, KB, P).transpose(0, 3, 2, 1).reshape(NCH, P, DM) for n in ("L0_ffn_w1", "L0_ffn_w3"))
    w2 = f["L0_ffn_w2"].reshape(DM, NCH, P).transpose(1, 2, 0)
    wff = np.concatenate([w1, w3, w2], axis=2)
    scales = np.concatenate([f["L0_ffn_w1_scale"], f["L0_ffn_w3_scale"], f["L0_ffn_w2_scale"].T], axis=1)
    small = np.concatenate([pairs(f["L0_xattn_bq"][None])[0], f["L0_xattn_bk"], f["L0_xattn_bv"], f["L0_xattn_bo"],
                            f["g_xattn"], f["g_ffn"], scales.reshape(-1)])[None]

    nc = bacc.Bacc("TRN2", target_bir_lowering=False, num_devices=1)
    arrays = {"x": f["x"], "ctxt": ctxt, "wproj": wproj, "small": small, "wff": wff}
    arrays = {k: np.ascontiguousarray(v) for k, v in arrays.items()}
    args = [nc.dram_tensor("in_" + k, v.shape, F32, kind="ExternalInput").ap() for k, v in arrays.items()]
    out = nc.dram_tensor("out", arrays["x"].shape, F32, kind="ExternalOutput").ap()
    build(nc, *args, out)
    r = run_bass_kernel_spmd(nc, [{"in_" + k: v for k, v in arrays.items()}], core_ids=[0])
    return r.results[0]["out"]
```

```python
from contextlib import ExitStack

import concourse.bass as bass
from concourse import mybir

F32 = mybir.dt.float32
F32R = mybir.dt.float32r
F16 = mybir.dt.float16
BF16 = mybir.dt.bfloat16
ALU = mybir.AluOpType
ACT = mybir.ActivationFunctionType
AX = mybir.AxisListType

P = 128
NBATCH = 8
DM = 512
KB = DM // P
HEADS = 32
KVH = 8
GJ = HEADS // KVH
DH = DM // HEADS
KVD = KVH * DH
PAIRS = KVH // 2
ROWS = 96
VC = 3 * DH + 1
FF = 1792
NCH = FF // P
HALVES = 2
HT = NBATCH // HALVES
TOK = HT * P
W13 = 2 * KB * P
CW = W13 + DM
NSC = CW // P
CHUNKS = HALVES * NCH
NRAW = 3
NEARLY = 5
NE, NL = 4, 4
EPS = 1e-5
SCALE = DH ** -0.5

KV0, Q0, O0 = 0, KB * 2 * KVD, KB * 2 * KVD + KB * DM
PW = O0 + KB * DM
QH = Q0 + KB * DM // 2
BQ, BK, BO = 0, DM, DM + 2 * KVD
BIAS = BO + DM
GATE, SC = BIAS, BIAS + 2
SMALL = SC + NCH * NSC


def build(nc, x, ctxt, wproj, small, wff, out):
    with ExitStack() as ctx:
        def sb(name, shape, dt=F32):
            return ctx.enter_context(nc.sbuf_tensor(name, shape, dt))

        def sem(name):
            return ctx.enter_context(nc.semaphore(name))

        def need(eng, s, n):
            if isinstance(n, int) and n <= 0:
                return
            eng.wait_ge(s, n)

        def r32(ap):
            return ap.bitcast(F32)

        X = sb("X", [P, NBATCH, DM])
        x2H = sb("x2H", [P, KB, NBATCH * P], F32R)
        x2L = sb("x2L", [P, KB, NBATCH * P], F32R)
        gsc = sb("gsc", [P, SMALL - GATE])
        tg = sb("tg", [P, 2])
        w13H = sb("w13H", [P, 2, W13], F32R)
        w13L = sb("w13L", [P, 2, W13], F32R)
        ps = ctx.enter_context(nc.psum_tensor("ps", [P, 8, 512], F32))
        W0, W1, W2, PVB = (ps[:, 4 + i, :] for i in range(4))
        G = (ps[:, 2, :], W0)
        U = (ps[:, 3, :], W2)
        Y = (ps[:, 0, :], ps[:, 1, :], PVB, W1)

        att = ctx.enter_context(ExitStack())

        def sa(name, shape, dt=F32):
            return att.enter_context(nc.sbuf_tensor(name, shape, dt))

        raw = sa("raw", [P, PW])
        WpH = sa("WpH", [P, PW], F32R)
        WpL = sa("WpL", [P, PW], F32R)
        PH = sa("PH", [P, KVH, GJ * P], F16)
        PL = sa("PL", [P, NL, GJ * P], F16)
        Vp = sa("Vp", [P, NBATCH, KVH, VC + 1], BF16)
        on = sa("on", [P, HEADS, DH])
        aTH = sa("aTH", [P, DM], F32R)
        ident = sa("ident", [P, P])
        sel = sa("sel", [P, 2, P])
        one2 = sa("one2", [P, P])
        Qtok = sa("Qtok", [P, PAIRS * GJ, 3, 32], F32R)
        Ktok = sa("Ktok", [P, PAIRS, 2, 3, 2, DH], F32R)
        Qst = sa("Qst", [P, PAIRS, GJ * P], F32R)
        Kst = sa("Kst", [P, PAIRS, 2, P], F32R)
        ctH = sa("ctH", [P, DM], F32R)
        ctL = sa("ctL", [P, DM], F32R)
        ct = sa("ct", [P, DM])
        xTH = sa("xTH", [P, DM], F32R)
        xTL = sa("xTL", [P, DM], F32R)
        xn = sa("xn", [P, DM])
        aTL = sa("aTL", [P, DM], F32R)
        x2n = sa("x2n", [P, DM])
        E = sa("E", [P, NE, GJ * P])
        identr = sa("identr", [P, P], F32R)
        neghalf, unit = sa("neghalf", [P, 1]), sa("unit", [P, 1])
        ones = sa("ones", [P, P], F32R)
        browf = sa("browf", [P, BIAS])
        brow = sa("brow", [P, BIAS], F32R)
        st1, mv1, ve1, rs1 = sa("st1", [P, 6]), sa("mv1", [P, 2]), sa("ve1", [P, 1]), sa("rs1", [P, 1])
        st2, mv2, ve2, rs2 = sa("st2", [P, 6]), sa("mv2", [P, 2]), sa("ve2", [P, 1]), sa("rs2", [P, 1])
        mx = sa("mx", [P, PAIRS, GJ, 2])
        Mtok = sa("Mtok", [P, PAIRS, GJ, 2, 2], F32R)
        vres = sa("vres", [P, KVH, DH])
        rden = sa("rden", [P, HEADS])
        att.close()

        wres = sb("wres", [P, NCH, CW])
        w2H = sb("w2H", [P, 2, DM], F32R)
        w2L = sb("w2L", [P, 2, DM], F32R)
        T = sb("T", [P, 2, TOK])
        A = sb("A", [P, 2, TOK])
        hf = sb("hf", [P, 2, TOK])
        hH = sb("hH", [P, 2, TOK], F32R)
        hL = sb("hL", [P, 2, TOK], F32R)

        wkv_in, wq_in, wq2_in, wo_in = sem("wkv_in"), sem("wq_in"), sem("wq2_in"), sem("wo_in")
        bias_in, gsc_in = sem("bias_in"), sem("gsc_in")
        x_in, xres_in, ct_in = sem("x_in"), sem("xres_in"), sem("ct_in")
        wff_in = [sem(f"wff_in{c}") for c in range(NCH)]
        consts = sem("consts")
        zeros = sem("zeros")
        selrows = sem("selrows")
        tanhg = sem("tanhg")
        browH_ok, brow_ok = sem("browH_ok"), sem("brow_ok")
        wpH_ok, wpL_ok, woL_ok = sem("wpH_ok"), sem("wpL_ok"), sem("woL_ok")
        stats1, mean1, ve1_ok, rs1_ok, xn_ok = (sem(n) for n in ("stats1", "mean1", "ve1_ok", "rs1_ok", "xn_ok"))
        stats2, mean2, ve2_ok, rs2_ok, x2n_ok = (sem(n) for n in ("stats2", "mean2", "ve2_ok", "rs2_ok", "x2n_ok"))
        ctH_ok, ctL_ok = sem("ctH_ok"), sem("ctL_ok")
        xT_ps, xTH_ok, xTL_ok = sem("xT_ps"), sem("xTH_ok"), sem("xTL_ok")
        kv_ps, q_ps = sem("kv_ps"), sem("q_ps")
        qtokH, qtokL, ktokH, ktokL = sem("qtokH"), sem("qtokL"), sem("ktokH"), sem("ktokL")
        v1_ok, r1_ok, v2_ok, v3_ok = sem("v1_ok"), sem("r1_ok"), sem("v2_ok"), sem("v3_ok")
        kst_ps, kst_ok, qst_ps, qst_ok = sem("kst_ps"), sem("kst_ok"), sem("qst_ps"), sem("qst_ok")
        s_ps, max_ok, mH_ok, mL_ok = sem("s_ps"), sem("max_ok"), sem("mH_ok"), sem("mL_ok")
        mT_ps, mrows = sem("mT_ps"), sem("mrows")
        st_ps, exp_ok, pL_ok = sem("st_ps"), sem("exp_ok"), sem("pL_ok")
        pv_ps, pv_read, on_ok = sem("pv_ps"), sem("pv_read"), sem("on_ok")
        aT_ps, aTH_ok, aTL_ok = sem("aT_ps"), sem("aTH_ok"), sem("aTL_ok")
        o_ps, x2_ok, xcopy_ok = sem("o_ps"), sem("x2_ok"), sem("xcopy_ok")
        x2T_ps, x2H_ok, x2L_ok = sem("x2T_ps"), sem("x2H_ok"), sem("x2L_ok")
        scaled = sem("scaled")
        w13H_ok, w13L_ok, w2H_ok, w2L_ok = sem("w13H_ok"), sem("w13L_ok"), sem("w2H_ok"), sem("w2L_ok")
        g_ps, u_ps, t_ok, a_ok, h_ok = sem("g_ps"), sem("u_ps"), sem("t_ok"), sem("a_ok"), sem("h_ok")
        hH_ok, hL_ok = sem("hH_ok"), sem("hL_ok")
        y_used = sem("y_used")
        y_ps, fin_ok, out_done = sem("y_ps"), sem("fin_ok"), sem("out_done")

        block = ctx.enter_context(nc.Block())

        def last(i):
            return isinstance(i, int) and i == NBATCH - 1

        def attention(eng, step):
            for i in (-1, 0):
                step(i, i + 2, i + 1, i if i > -1 else None, None)
            with eng.Fori(1, NBATCH - 2) as i:
                step(i, i + 2, i + 1, i, i - 1)
            for i in (NBATCH - 2, NBATCH - 1):
                step(i, None, i + 1 if i < NBATCH - 1 else None, i, i - 1)

        def feed_forward(eng, ffn):
            for h in range(HALVES):
                c0 = h * NCH
                if h:
                    ffn(h, c0, 0, 0, 1)
                ffn(h, c0 + 1, 1, 1, 2 if h else None)
                with eng.Fori(1, NCH // 2 - 1) as p:
                    ffn(h, c0 + 2 * p, 2 * p, 0, 2 * p + 1)
                    ffn(h, c0 + 2 * p + 1, 2 * p + 1, 1, 2 * p + 2)
                ffn(h, c0 + NCH - 2, NCH - 2, 0, NCH - 1)
                ffn(h, c0 + NCH - 1, NCH - 1, 1, 0 if h < HALVES - 1 else None)

        @block.sync
        def _(sp):
            sp.dma_start(xn[:], x[0]).then_inc(x_in, 16)
            sp.dma_start(raw[:, KV0:Q0], wproj[:, KV0:Q0]).then_inc(wkv_in, 16)
            sp.dma_start(raw[:, Q0:QH], wproj[:, Q0:QH]).then_inc(wq_in, 16)
            sp.dma_start(raw[:, QH:O0], wproj[:, QH:O0]).then_inc(wq2_in, 16)
            sp.dma_start(browf[0:33, :], small[:, 0:BIAS].broadcast_to([33, BIAS])).then_inc(bias_in, 16)
            sp.wait_ge(xT_ps, 1)
            sp.dma_start(xn[:], x[1]).then_inc(x_in, 16)
            sp.dma_start(raw[:, O0:PW], wproj[:, O0:PW]).then_inc(wo_in, 16)
            sp.wait_ge(ctL_ok, 1)
            sp.dma_start(ct[:], ctxt[1]).then_inc(ct_in, 16)
            sp.dma_start(gsc[:], small[:, GATE:SMALL].broadcast_to([P, SMALL - GATE])).then_inc(gsc_in, 16)
            sp.dma_start(X[:], x.rearrange("b p n -> p b n")).then_inc(xres_in, 16)
            with sp.Fori(2, NBATCH) as b:
                sp.wait_ge(ctL_ok, b)
                sp.dma_start(ct[:], ctxt[b]).then_inc(ct_in, 16)
                sp.wait_ge(xT_ps, b)
                sp.dma_start(xn[:], x[b]).then_inc(x_in, 16)
            sp.wait_ge(wpL_ok, 3)
            sp.wait_ge(woL_ok, 1)
            for c in range(NCH):
                if c == NRAW:
                    sp.wait_ge(kv_ps, NBATCH)
                    sp.wait_ge(q_ps, NBATCH)
                if c == NEARLY:
                    sp.wait_ge(x2L_ok, NBATCH)
                sp.dma_start(wres[:, c, :], wff[c]).then_inc(wff_in[c], 16)
            with sp.Fori(0, HT) as t:
                sp.wait_ge(fin_ok, t + 1)
                sp.dma_start(out[t], X[:, t, :]).then_inc(out_done, 16)
            for t in range(HT, NBATCH, 2):
                sp.wait_ge(fin_ok, t + 1)
                sp.dma_start(out[t], X[:, t, :]).then_inc(out_done, 16)
            sp.wait_ge(out_done, 16 * NBATCH)

        @block.gpsimd
        def _(pool):
            pool.memset(neghalf[:], -0.5).then_inc(consts, 1)
            pool.memset(ident[:], 0.0).then_inc(consts, 1)
            pool.memset(one2[:], 0.0).then_inc(consts, 1)
            pool.memset(sel[:], 1.0).then_inc(consts, 1)
            pool.wait_ge(consts, 4)
            pool.affine_select(out=ident[:], in_=ident[:], compare_op=ALU.not_equal, fill=1.0, base=0,
                               pattern=[[-1, P]], channel_multiplier=1).then_inc(consts, 1)
            pool.affine_select(out=one2[:], in_=one2[:], compare_op=ALU.not_equal, fill=1.0, base=0,
                               pattern=[[0, P]], channel_multiplier=1).then_inc(consts, 1)
            pool.affine_select(out=sel[:], in_=sel[:], compare_op=ALU.is_ge, fill=0.0, base=-ROWS,
                               pattern=[[-2, 2], [0, P]], channel_multiplier=1).then_inc(consts, 1)
            pool.wait_ge(consts, 7)
            pool.affine_select(out=one2[:], in_=one2[:], compare_op=ALU.not_equal, fill=1.0, base=-32,
                               pattern=[[0, P]], channel_multiplier=1).then_inc(consts, 1)
            pool.affine_select(out=sel[:], in_=sel[:], compare_op=ALU.is_ge, fill=0.0, base=ROWS + 1,
                               pattern=[[2, 2], [0, P]], channel_multiplier=-1).then_inc(consts, 1)

            pool.memset(unit[:], 1.0).then_inc(consts, 1)
            pool.memset(Vp[:, :, :, 3 * DH:VC], 1.0).then_inc(consts, 1)

            pool.wait_ge(consts, 11)
            pool.wait_ge(ve1_ok, 1)
            pool.tensor_tensor(rs1[:], ve1[:], neghalf[:], ALU.pow).then_inc(rs1_ok, 1)
            pool.wait_ge(ctH_ok, 1)
            pool.tensor_tensor(ctL[:], ct[:], r32(ctH[:]), ALU.subtract).then_inc(ctL_ok, 1)

            def scale(c):
                w = wres[:, c, :].rearrange("p (a n) -> p a n", n=P)
                v = gsc[:, 2 + c * NSC:2 + (c + 1) * NSC].unsqueeze(2).broadcast_to([P, NSC, P])
                pool.wait_ge(wff_in[c], 16)
                pool.tensor_tensor(w, w, v, ALU.mult).then_inc(scaled, 1)

            def step(i, a, f, b, l):
                def low(g):
                    pool.wait_ge(exp_ok, 2 * (8 * b + g + 1))
                    need(pool, pv_ps, 8 * b + g - NL + 1)
                    pool.tensor_tensor(PL[:, g % NL, :], E[:, g % NE, :], PH[:, g, :], ALU.subtract).then_inc(pL_ok, 1)

                if a is not None:
                    pool.wait_ge(ct_in, 16 * (a + 1))
                    need(pool, kv_ps, a)
                    pool.tensor_tensor(ctH[:], ct[:], unit[:].broadcast_to([P, DM]), ALU.mult).then_inc(ctH_ok, 1)
                if isinstance(i, int) and i >= NBATCH - 2:
                    if i == NBATCH - 2:
                        pool.wait_ge(gsc_in, 16)
                    scale(i - NBATCH + 2)
                if b is not None:
                    low(0)
                    low(1)
                if a is not None:
                    need(pool, xn_ok, a)
                    pool.wait_ge(ve1_ok, a + 1)
                    pool.tensor_tensor(rs1[:], ve1[:], neghalf[:], ALU.pow).then_inc(rs1_ok, 1)
                if b is not None:
                    low(2)
                    low(3)
                    low(4)
                if l is not None:
                    need(pool, x2n_ok, l)
                    pool.wait_ge(ve2_ok, l + 1)
                    pool.tensor_tensor(rs2[:], ve2[:], neghalf[:], ALU.pow).then_inc(rs2_ok, 1)
                if b is not None:
                    low(5)
                if a is not None:
                    pool.wait_ge(ctH_ok, a + 1)
                    pool.tensor_tensor(ctL[:], ct[:], r32(ctH[:]), ALU.subtract).then_inc(ctL_ok, 1)
                if isinstance(i, int) and i == -1:
                    pool.wait_ge(wpH_ok, 4)
                    pool.tensor_tensor(WpL[:, O0:PW], raw[:, O0:PW], r32(WpH[:, O0:PW]), ALU.subtract).then_inc(woL_ok, 1)
                if b is not None:
                    low(6)
                    low(7)

            attention(pool, step)

            scale(2)
            pool.wait_ge(ve2_ok, NBATCH)
            pool.wait_ge(x2n_ok, NBATCH - 1)
            pool.tensor_tensor(rs2[:], ve2[:], neghalf[:], ALU.pow).then_inc(rs2_ok, 1)
            for c in range(3, NCH):
                scale(c)

        @block.scalar
        def _(act):
            act.dma_start(ct[:], ctxt[0]).then_inc(ct_in, 16)

            def weights_high(s, c0, c1):
                act.wait_ge(s, 16)
                act.activation(WpH[:, c0:c1], raw[:, c0:c1], ACT.Copy).then_inc(wpH_ok, 1)

            def x_high(a):
                act.wait_ge(xT_ps, a + 1)
                need(act, q_ps, a)
                act.activation(xTH[:], W1, ACT.Copy).then_inc(xTH_ok, 1)

            def k_high(a):
                act.wait_ge(kv_ps, a + 1)
                need(act, ktokL, 2 * a)
                for gg in range(2):
                    act.activation(Ktok[:, :, gg, 0:2, gg, :],
                                   W0[:, 0:KVD].rearrange("p (a g d) -> p a g d", a=PAIRS, g=2)[:, :, gg, :]
                                   .unsqueeze(2).broadcast_to([P, PAIRS, 2, DH]), ACT.Copy).then_inc(ktokH, 1)

            def q_high(a):
                act.wait_ge(q_ps, a + 1)
                need(act, qst_ps, 4 * a)
                need(act, qtokL, a)
                act.activation(Qtok[:, :, 0:3:2, :], W2.rearrange("p (a d) -> p a d", d=32)
                               .unsqueeze(2).broadcast_to([P, PAIRS * GJ, 2, 32]), ACT.Copy).then_inc(qtokH, 1)

            def o_high(l):
                act.wait_ge(aT_ps, l + 1)
                need(act, o_ps, l)
                act.activation(aTH[:], W1, ACT.Copy).then_inc(aTH_ok, 1)

            def x2_high(l):
                act.wait_ge(x2T_ps, l + 1)
                act.activation(x2H[:, :, bass.ds(l * P, P)], W1.rearrange("p (k n) -> p k n", k=KB),
                               ACT.Copy).then_inc(x2H_ok, 1)

            def split13(c, n, s):
                act.wait_ge(scaled, n + 1)
                need(act, u_ps, c - 1)
                act.activation(w13H[:, s, :], wres[:, n, 0:W13], ACT.Copy).then_inc(w13H_ok, 1)

            act.wait_ge(ct_in, 16)
            act.activation(ctH[:], ct[:], ACT.Copy).then_inc(ctH_ok, 1)
            weights_high(wkv_in, KV0, Q0)
            weights_high(wq_in, Q0, QH)
            x_high(0)
            weights_high(wq2_in, QH, O0)
            act.wait_ge(bias_in, 16)
            act.activation(brow[0:33, :], browf[0:33, :], ACT.Copy).then_inc(browH_ok, 1)
            k_high(0)
            q_high(0)

            def step(i, a, f, b, l):
                def exps(g):
                    act.wait_ge(st_ps, 8 * b + g + 1)
                    need(act, pL_ok, 8 * b + g - NE + 1)
                    act.activation(E[:, g % NE, :], ps[:, g % 2, :], ACT.Exp, scale=SCALE).then_inc(exp_ok, 1)
                    need(act, pv_ps, 8 * b + g - KVH + 1)
                    act.activation(PH[:, g, :], ps[:, g % 2, :], ACT.Exp, scale=SCALE).then_inc(exp_ok, 1)

                def stack_k(h):
                    act.wait_ge(kst_ps, 4 * f + h + 1)
                    act.activation(Kst[0:ROWS, h, :, :], W0[0:ROWS, 0:2 * P].rearrange("p (g k) -> p g k", g=2),
                                   ACT.Copy).then_inc(kst_ok, 1)

                def stack_q(h):
                    act.wait_ge(qst_ps, 4 * f + h + 1)
                    act.activation(Qst[0:ROWS, h, :], W1[0:ROWS, :], ACT.Copy).then_inc(qst_ok, 1)

                def max_rows(n, h):
                    act.wait_ge(mT_ps, 4 * n + h + 1)
                    act.activation(Qst[ROWS:ROWS + 4, h, :], (W1 if h == 1 else W0)[0:4, :], ACT.Copy).then_inc(mrows, 1)

                if b is not None:
                    max_rows(b, 1)
                    exps(0)
                if f is not None:
                    stack_q(0)
                    stack_k(0)
                if b is not None:
                    exps(1)
                if l is not None:
                    o_high(l)
                if b is not None:
                    max_rows(b, 2)
                if isinstance(i, int) and i == NBATCH - 2:
                    split13(0, 0, 0)
                if b is not None:
                    exps(2)
                if f is not None:
                    stack_q(1)
                if b is not None:
                    exps(3)
                if f is not None:
                    stack_k(1)
                if a is not None:
                    x_high(a)
                if isinstance(i, int) and i == -1:
                    weights_high(wo_in, O0, PW)
                if b is not None:
                    exps(4)
                    max_rows(b, 3)
                    exps(5)
                if f is not None:
                    stack_k(2)
                    stack_q(2)
                if b is not None:
                    exps(6)
                if f is not None:
                    max_rows(f, 0)
                if l is not None:
                    x2_high(l)
                if b is not None:
                    exps(7)
                if f is not None:
                    stack_k(3)
                if a is not None:
                    q_high(a)
                if f is not None:
                    stack_q(3)
                if isinstance(i, int) and i == -1:
                    act.wait_ge(gsc_in, 16)
                    act.activation(tg[:], gsc[:, 0:2], ACT.Tanh).then_inc(tanhg, 1)
                if a is not None:
                    k_high(a)

            attention(act, step)

            def tanh(c, s):
                act.wait_ge(g_ps, c + 1)
                need(act, a_ok, c - 1)
                act.activation(T[:, s, :], G[s], ACT.Tanh, scale=0.5).then_inc(t_ok, 1)

            def w2_high(h, c, n, s):
                need(act, y_used, c - 1 - h)
                act.activation(w2H[:, s, :], wres[:, n, W13:CW], ACT.Copy).then_inc(w2H_ok, 1)

            def h_high(c, s):
                act.wait_ge(h_ok, c + 1)
                act.activation(hH[:, s, :], hf[:, s, :], ACT.Copy).then_inc(hH_ok, 1)

            def ffn(h, c, n, s, ahead):
                if ahead is not None:
                    split13(c + 1, ahead, 1 - s)
                tanh(c, s)
                w2_high(h, c, n, s)
                h_high(c, s)

            split13(1, 1, 1)
            tanh(0, 0)
            o_high(NBATCH - 1)
            w2_high(0, 0, 0, 0)
            h_high(0, 0)
            split13(2, 2, 0)
            x2_high(NBATCH - 1)
            feed_forward(act, ffn)
            for t in range(HT + 1, NBATCH, 2):
                act.wait_ge(fin_ok, t + 1)
                act.dma_start(out[t], X[:, t, :]).then_inc(out_done, 16)

        @block.vector
        def _(dve):
            dve.memset(r32(Ktok[:]), 0.0).then_inc(zeros, 1)
            dve.memset(r32(Qst[ROWS:P, 0:2, :]), 0.0).then_inc(zeros, 1)

            def weights_low(n, c0, c1):
                dve.wait_ge(wpH_ok, n)
                dve.tensor_tensor(WpL[:, c0:c1], raw[:, c0:c1], r32(WpH[:, c0:c1]), ALU.subtract).then_inc(wpL_ok, 1)

            def stats(a):
                dve.wait_ge(x_in, 16 * (a + 1))
                dve.bn_stats(st1[:], xn[:]).then_inc(stats1, 1)
                dve.wait_ge(stats1, a + 1)

            def variance(a):
                dve.bn_aggr(mv1[:], st1[:]).then_inc(mean1, 1)

            def epsilon(a):
                dve.wait_ge(mean1, a + 1)
                dve.tensor_scalar(ve1[:], mv1[:, 1:2], EPS, None, ALU.add).then_inc(ve1_ok, 1)

            def normalise(a):
                dve.wait_ge(rs1_ok, a + 1)
                dve.tensor_scalar(xn[:], xn[:], mv1[:, 0:1], rs1[:, 0:1], ALU.subtract, ALU.mult).then_inc(xn_ok, 1)

            def x_low(a):
                dve.wait_ge(xTH_ok, a + 1)
                dve.tensor_tensor(xTL[:], W1, r32(xTH[:]), ALU.subtract).then_inc(xTL_ok, 1)

            def k_low(a):
                dve.wait_ge(ktokH, 2 * a + 2)
                for gg in range(2):
                    dve.tensor_tensor(Ktok[:, :, gg, 2, gg, :],
                                      W0[:, 0:KVD].rearrange("p (a g d) -> p a g d", a=PAIRS, g=2)[:, :, gg, :],
                                      r32(Ktok[:, :, gg, 0, gg, :]), ALU.subtract).then_inc(ktokL, 1)

            def v_first(a):
                dve.tensor_copy(Vp[:, a, :, 0:DH],
                                W0[:, KVD:2 * KVD].rearrange("p (g d) -> p g d", g=KVH)).then_inc(v1_ok, 1)

            def v_rest(a):
                dve.wait_ge(v1_ok, a + 1)
                dve.tensor_tensor(vres[:], W0[:, KVD:2 * KVD].rearrange("p (g d) -> p g d", g=KVH), Vp[:, a, :, 0:DH],
                                  ALU.subtract).then_inc(r1_ok, 1)

            def q_low(a):
                dve.wait_ge(qtokH, a + 1)
                dve.tensor_tensor(Qtok[:, :, 1, :], W2.rearrange("p (a d) -> p a d", d=32),
                                  r32(Qtok[:, :, 0, :]), ALU.subtract).then_inc(qtokL, 1)

            def pv_reduce(b, q):
                dve.wait_ge(pv_ps, 8 * b + 2 * q + 2)
                if q == 0:
                    need(dve, aT_ps, b)
                v = PVB[:, 0:8 * VC].rearrange("p (h c) -> p h c", c=VC)
                dve.tensor_reduce(on[:, 8 * q:8 * q + 8, :], v[:, :, 0:3 * DH].rearrange("p h (t d) -> p h d t", t=3),
                                  AX.X, ALU.add).then_inc(pv_read, 1)
                dve.reciprocal(rden[:, 8 * q:8 * q + 8], v[:, :, 3 * DH]).then_inc(pv_read, 1)

            def pv_norm(b, q):
                o = on[:, 8 * q:8 * q + 8, :]
                dve.wait_ge(pv_read, 2 * (4 * b + q) + 2)
                dve.tensor_tensor(o, o, rden[:, 8 * q:8 * q + 8].unsqueeze(2).broadcast_to([P, 8, DH]),
                                  ALU.mult).then_inc(on_ok, 1)

            def max_reduce(f, h):
                dve.wait_ge(s_ps, 4 * f + h + 1)
                dve.tensor_reduce(mx[:, h, :, :], ps[:, 2:4, :].rearrange("p b (j g k) -> p (b j) g k", j=2, g=2),
                                  AX.X, ALU.max).then_inc(max_ok, 1)

            def max_high(f, h):
                dve.wait_ge(max_ok, 4 * f + h + 1)
                need(dve, mT_ps, 4 * (f - 1) + h + 1)
                dve.tensor_scalar(Mtok[:, h, :, :, 0], mx[:, h, :, :], -1.0, None, ALU.mult).then_inc(mH_ok, 1)

            def max_low(f, h):
                dve.wait_ge(mH_ok, 4 * f + h + 1)
                dve.scalar_tensor_tensor(out=Mtok[:, h, :, :, 1], in0=mx[:, h, :, :], scalar=-1.0,
                                         in1=r32(Mtok[:, h, :, :, 0]), op0=ALU.mult, op1=ALU.subtract).then_inc(mL_ok, 1)

            def attention_low(l):
                dve.wait_ge(aTH_ok, l + 1)
                dve.tensor_tensor(aTL[:], W1, r32(aTH[:]), ALU.subtract).then_inc(aTL_ok, 1)

            def residual(l):
                dve.wait_ge(o_ps, l + 1)
                if isinstance(l, int) and l == 0:
                    dve.wait_ge(xres_in, 16)
                    dve.wait_ge(tanhg, 1)
                need(dve, x2T_ps, l)
                dve.scalar_tensor_tensor(out=x2n[:], in0=W2, scalar=tg[:, 0:1], in1=X[:, l, :],
                                         op0=ALU.mult, op1=ALU.add).then_inc(x2_ok, 1)

            def statistics2(l):
                dve.wait_ge(x2_ok, l + 1)
                dve.bn_stats(st2[:], x2n[:]).then_inc(stats2, 1)
                dve.wait_ge(stats2, l + 1)

            def keep_x2(l):
                dve.tensor_copy(X[:, l, :], x2n[:]).then_inc(xcopy_ok, 1)

            def variance2(l):
                dve.bn_aggr(mv2[:], st2[:]).then_inc(mean2, 1)

            def epsilon2(l):
                dve.wait_ge(mean2, l + 1)
                dve.tensor_scalar(ve2[:], mv2[:, 1:2], EPS, None, ALU.add).then_inc(ve2_ok, 1)

            def normalise2(l):
                dve.wait_ge(rs2_ok, l + 1)
                dve.wait_ge(xcopy_ok, l + 1)
                dve.tensor_scalar(x2n[:], x2n[:], mv2[:, 0:1], rs2[:, 0:1], ALU.subtract, ALU.mult).then_inc(x2n_ok, 1)

            def x2_low(l):
                dve.wait_ge(x2H_ok, l + 1)
                dve.tensor_tensor(x2L[:, :, bass.ds(l * P, P)], W1.rearrange("p (k n) -> p k n", k=KB),
                                  r32(x2H[:, :, bass.ds(l * P, P)]), ALU.subtract).then_inc(x2L_ok, 1)

            def split13(c, n, s):
                dve.wait_ge(w13H_ok, c + 1)
                dve.tensor_tensor(w13L[:, s, :], wres[:, n, 0:W13], r32(w13H[:, s, :]), ALU.subtract).then_inc(w13L_ok, 1)

            dve.wait_ge(consts, 8)
            dve.tensor_copy(identr[:], ident[:]).then_inc(selrows, 1)
            dve.tensor_copy(ones[:], one2[:]).then_inc(selrows, 1)
            stats(0)
            variance(0)
            epsilon(0)
            dve.memset(r32(Qst[ROWS:P, 2:4, :]), 0.0).then_inc(zeros, 1)
            normalise(0)
            weights_low(1, KV0, Q0)
            weights_low(2, Q0, QH)
            x_low(0)
            weights_low(3, QH, O0)
            dve.wait_ge(browH_ok, 1)
            dve.tensor_tensor(brow[32:33, :], browf[32:33, :], r32(brow[32:33, :]), ALU.subtract).then_inc(brow_ok, 1)
            k_low(0)
            v_first(0)
            v_rest(0)
            dve.wait_ge(consts, 11)
            dve.tensor_copy(Kst[ROWS:P, :, :, :], sel[ROWS:P, :, :].unsqueeze(1)
                            .broadcast_to([P - ROWS, PAIRS, 2, P])).then_inc(selrows, 1)
            q_low(0)

            def step(i, a, f, b, l):
                if l is not None:
                    pv_reduce(l, 3)
                    pv_norm(l, 3)
                if b is not None:
                    max_reduce(b, 3)
                if a is not None:
                    stats(a)
                if l is not None:
                    attention_low(l)
                if f is not None:
                    dve.wait_ge(r1_ok, f + 1)
                    dve.tensor_copy(Vp[:, f, :, DH:2 * DH], vres[:]).then_inc(v2_ok, 1)
                if b is not None:
                    max_high(b, 3)
                if a is not None:
                    variance(a)
                    epsilon(a)
                if b is not None:
                    max_low(b, 3)
                if isinstance(i, int) and i == NBATCH - 2:
                    split13(0, 0, 0)
                if a is not None:
                    normalise(a)
                if f is not None:
                    max_reduce(f, 0)
                if b is not None:
                    pv_reduce(b, 0)
                if a is not None:
                    x_low(a)
                if f is not None:
                    dve.wait_ge(v2_ok, f + 1)
                    dve.tensor_tensor(Vp[:, f, :, 2 * DH:3 * DH], vres[:], Vp[:, f, :, DH:2 * DH],
                                      ALU.subtract).then_inc(v3_ok, 1)
                if l is not None:
                    residual(l)
                    statistics2(l)
                if f is not None:
                    max_high(f, 0)
                if l is not None:
                    variance2(l)
                if f is not None:
                    max_low(f, 0)
                if l is not None:
                    epsilon2(l)
                    keep_x2(l)
                if b is not None:
                    pv_reduce(b, 1)
                if l is not None:
                    normalise2(l)
                if f is not None:
                    max_reduce(f, 1)
                    max_high(f, 1)
                if b is not None:
                    pv_norm(b, 0)
                if l is not None:
                    x2_low(l)
                if f is not None:
                    max_low(f, 1)
                if b is not None:
                    pv_norm(b, 1)
                    pv_reduce(b, 2)
                if f is not None:
                    max_reduce(f, 2)
                if b is not None:
                    pv_norm(b, 2)
                if a is not None:
                    q_low(a)
                    k_low(a)
                if f is not None:
                    max_high(f, 2)
                if a is not None:
                    v_first(a)
                if f is not None:
                    max_low(f, 2)
                if a is not None:
                    v_rest(a)

            attention(dve, step)

            def final(h):
                for t in range(HT):
                    n = h * HT + t
                    dve.wait_ge(y_ps, n + 1)
                    dve.scalar_tensor_tensor(out=X[:, n, :], in0=Y[t], scalar=tg[:, 1:2], in1=X[:, n, :],
                                             op0=ALU.mult, op1=ALU.add).then_inc(fin_ok, 1)

            def silu(c, s):
                dve.wait_ge(t_ok, c + 1)
                need(dve, h_ok, c - 1)
                dve.scalar_tensor_tensor(out=A[:, s, :], in0=T[:, s, :], scalar=1.0, in1=G[s],
                                         op0=ALU.add, op1=ALU.mult).then_inc(a_ok, 1)

            def gated(c, s):
                dve.wait_ge(u_ps, c + 1)
                dve.wait_ge(a_ok, c + 1)
                need(dve, hL_ok, c - 1)
                dve.scalar_tensor_tensor(out=hf[:, s, :], in0=A[:, s, :], scalar=0.5, in1=U[s],
                                         op0=ALU.mult, op1=ALU.mult).then_inc(h_ok, 1)

            def w2_low(c, n, s):
                dve.wait_ge(w2H_ok, c + 1)
                dve.tensor_tensor(w2L[:, s, :], wres[:, n, W13:CW], r32(w2H[:, s, :]), ALU.subtract).then_inc(w2L_ok, 1)

            def h_low(c, s):
                dve.wait_ge(hH_ok, c + 1)
                dve.tensor_tensor(hL[:, s, :], hf[:, s, :], r32(hH[:, s, :]), ALU.subtract).then_inc(hL_ok, 1)

            def ffn(h, c, n, s, ahead):
                if ahead is not None:
                    split13(c + 1, ahead, 1 - s)
                if isinstance(c, int) and c == NCH:
                    final(0)
                silu(c, s)
                gated(c, s)
                w2_low(c, n, s)
                h_low(c, s)

            l = NBATCH - 1
            split13(1, 1, 1)
            pv_reduce(l, 3)
            pv_norm(l, 3)
            silu(0, 0)
            attention_low(l)
            gated(0, 0)
            w2_low(0, 0, 0)
            residual(l)
            statistics2(l)
            keep_x2(l)
            variance2(l)
            epsilon2(l)
            h_low(0, 0)
            normalise2(l)
            split13(2, 2, 0)
            x2_low(l)
            feed_forward(dve, ffn)
            final(1)

        @block.tensor
        def _(pe):
            def three(out_ap, aH, aL, bH, bL, start, stop):
                pe.matmul(out_ap, aH, bH, start=start, stop=False)
                pe.matmul(out_ap, aH, bL, start=False, stop=False)
                return pe.matmul(out_ap, aL, bH, start=False, stop=stop)

            def turn(out_ap, in_ap):
                if in_ap.dtype == F32R:
                    return pe.matmul(out_ap.bitcast(F32R), in_ap, identr[:], start=True, stop=True, is_transpose=True)
                return pe.matmul(out_ap, in_ap, ident[:], start=True, stop=True, is_transpose=True)

            def turn4(bank, src):
                for k in range(KB):
                    m = turn(bank[:, k * P:(k + 1) * P], src[:, k * P:(k + 1) * P])
                return m

            def project(bank, width, H, L, w0, blocks):
                for k in blocks:
                    c = slice(w0 + k * width, w0 + (k + 1) * width)
                    three(bank[:, 0:width], H[:, k * P:(k + 1) * P], L[:, k * P:(k + 1) * P],
                          WpH[:, c], WpL[:, c], k == 0, False)

            def add_bias(bank, width, b0):
                return pe.matmul(bank[:, 0:width], ones[0:33, :], brow[0:33, b0:b0 + width], start=False, stop=True)

            def g_or_u(c, s, h, which, blocks=range(KB)):
                m0, bank, done = ((0, G[s], g_ps), (KB, U[s], u_ps))[which]
                for k in blocks:
                    w = slice((m0 + k) * P, (m0 + k + 1) * P)
                    t = slice(h * TOK, (h + 1) * TOK)
                    m = three(bank, w13H[:, s, w], w13L[:, s, w], x2H[:, k, t], x2L[:, k, t], k == 0, k == KB - 1)
                if k == KB - 1:
                    m.then_inc(done, 1)

            def values(b, g):
                pe.wait_ge(pL_ok, 8 * b + g + 1)
                if g % 2 == 0:
                    need(pe, pv_read, 2 * (4 * b + g // 2))
                for j in range(GJ):
                    h = (g % 2) * GJ + j
                    o = PVB[:, h * VC:(h + 1) * VC]
                    v = Vp[:, b, g, 0:VC]
                    pe.matmul(o, PH[:, g, j * P:(j + 1) * P], v, start=True, stop=False)
                    m = pe.matmul(o, PL[:, g % NL, j * P:(j + 1) * P], v, start=False, stop=True)
                m.then_inc(pv_ps, 1)

            pe.wait_ge(consts, 11)
            pe.wait_ge(xn_ok, 1)
            turn4(W1, xn).then_inc(xT_ps, 1)
            pe.wait_ge(ctL_ok, 1)
            pe.wait_ge(wpL_ok, 1)
            project(W0, 2 * KVD, ctH, ctL, KV0, range(KB))
            pe.wait_ge(xTL_ok, 1)
            pe.wait_ge(wpL_ok, 2)
            project(W2, DM, xTH, xTL, Q0, range(2))
            pe.wait_ge(selrows, 2)
            pe.wait_ge(brow_ok, 1)
            add_bias(W0, 2 * KVD, BK).then_inc(kv_ps, 1)
            pe.wait_ge(wpL_ok, 3)
            project(W2, DM, xTH, xTL, Q0, range(2, KB))
            add_bias(W2, DM, BQ).then_inc(q_ps, 1)
            pe.wait_ge(zeros, 3)

            def step(i, a, f, b, l):
                def scores_t(g):
                    pe.wait_ge(mrows, 4 * b + g // 2 + 1)
                    need(pe, exp_ok, 2 * (8 * b + g - 1))
                    pe.matmul(ps[:, g % 2, :], Kst[:, g // 2, g % 2, :], Qst[:, g // 2, :],
                              start=True, stop=True).then_inc(st_ps, 1)

                def stack_k(h):
                    for gg in range(2):
                        m = turn(W0[0:ROWS, gg * P:(gg + 1) * P],
                                 Ktok[:, h, gg, :, :, :].rearrange("p t g d -> p (t g d)"))
                    m.then_inc(kst_ps, 1)

                def stack_q(h):
                    for j in range(GJ):
                        m = turn(W1[0:ROWS, j * P:(j + 1) * P],
                                 Qtok[:, h * GJ + j, :, :].rearrange("p t d -> p (t d)"))
                    m.then_inc(qst_ps, 1)

                def scores(f, h):
                    pe.wait_ge(kst_ok, 4 * f + h + 1)
                    pe.wait_ge(qst_ok, 4 * f + h + 1)
                    need(pe, max_ok, 4 * f + h)
                    for j in range(GJ):
                        m = pe.matmul(ps[:, 2 + j // 2, (j % 2) * 2 * P:(j % 2 + 1) * 2 * P],
                                      Qst[0:ROWS, h, j * P:(j + 1) * P], Kst[0:ROWS, h, :, :], start=True, stop=True)
                    m.then_inc(s_ps, 1)

                def rows_max(n, h, bank):
                    pe.wait_ge(mL_ok, 4 * n + h + 1)
                    for j in range(GJ):
                        m = turn(bank[0:4, j * P:(j + 1) * P], Mtok[:, h, j, :, :].rearrange("p g t -> p (g t)"))
                    m.then_inc(mT_ps, 1)

                if b is not None:
                    pe.wait_ge(qst_ok, 4 * b + 4)
                    rows_max(b, 1, W1)
                if l is not None:
                    values(l, 6)
                if b is not None:
                    if isinstance(b, int) and b == 0:
                        pe.wait_ge(selrows, 3)
                    scores_t(0)
                if l is not None:
                    values(l, 7)
                if b is not None:
                    scores_t(1)
                if f is not None:
                    pe.wait_ge(qtokL, f + 1)
                    if b is not None:
                        pe.wait_ge(mrows, 4 * b + 2)
                    else:
                        pe.wait_ge(xTL_ok, 1)
                    stack_q(0)
                if b is not None:
                    scores(b, 3)
                if f is not None:
                    pe.wait_ge(ktokL, 2 * f + 2)
                    pe.wait_ge(r1_ok, f + 1)
                    stack_k(0)
                if b is not None:
                    scores_t(2)
                if l is not None:
                    pe.wait_ge(on_ok, 4 * l + 4)
                    if f is not None:
                        pe.wait_ge(qst_ok, 4 * f + 1)
                    elif b is not None:
                        pe.wait_ge(mrows, 4 * b + 2)
                    else:
                        pe.wait_ge(x2L_ok, l)
                    for k in range(KB):
                        m = turn(W1[:, k * P:(k + 1) * P], on[:, k * 8:(k + 1) * 8, :].rearrange("p h d -> p (h d)"))
                    m.then_inc(aT_ps, 1)
                if b is not None:
                    if f is not None:
                        pe.wait_ge(kst_ok, 4 * f + 1)
                    rows_max(b, 2, W0)
                if f is not None:
                    scores(f, 0)
                if b is not None:
                    scores_t(3)
                    pe.wait_ge(v3_ok, b + 1)
                    values(b, 0)
                if f is not None:
                    if b is not None:
                        pe.wait_ge(mrows, 4 * b + 3)
                    else:
                        pe.wait_ge(kst_ok, 4 * f + 1)
                    stack_k(1)
                    if l is not None:
                        pe.wait_ge(aTL_ok, l + 1)
                    else:
                        pe.wait_ge(qst_ok, 4 * f + 1)
                    stack_q(1)
                if l is not None:
                    pe.wait_ge(aTL_ok, l + 1)
                    pe.wait_ge(woL_ok, 1)
                    project(W2, DM, aTH, aTL, O0, range(2))
                if b is not None:
                    values(b, 1)
                    scores_t(4)
                if a is not None:
                    pe.wait_ge(xn_ok, a + 1)
                    if f is not None:
                        pe.wait_ge(qst_ok, 4 * f + 2)
                    for k in range(KB):
                        m = turn(W1[:, k * P:(k + 1) * P], xn[:, k * P:(k + 1) * P])
                    m.then_inc(xT_ps, 1)
                if l is not None:
                    project(W2, DM, aTH, aTL, O0, range(2, KB))
                    add_bias(W2, DM, BO).then_inc(o_ps, 1)
                if b is not None:
                    if f is not None:
                        pe.wait_ge(kst_ok, 4 * f + 2)
                    else:
                        pe.wait_ge(mrows, 4 * b + 3)
                    rows_max(b, 3, W0)
                    scores_t(5)
                    values(b, 2)
                    values(b, 3)
                if f is not None:
                    scores(f, 1)
                    if a is not None:
                        pe.wait_ge(xTL_ok, a + 1)
                    else:
                        pe.wait_ge(qst_ok, 4 * f + 2)
                    stack_q(2)
                    if b is not None:
                        pe.wait_ge(mrows, 4 * b + 4)
                    else:
                        pe.wait_ge(kst_ok, 4 * f + 2)
                    stack_k(2)
                if b is not None:
                    scores_t(6)
                if last(i):
                    pe.wait_ge(w13L_ok, 1)
                    pe.wait_ge(max_ok, 4 * NBATCH)
                    g_or_u(0, 0, 0, 0, range(2))
                if a is not None:
                    pe.wait_ge(xTL_ok, a + 1)
                    if l is not None:
                        pe.wait_ge(x2_ok, l + 1)
                    project(W2, DM, xTH, xTL, Q0, range(2))
                if b is not None:
                    scores_t(7)
                if last(i):
                    g_or_u(0, 0, 0, 0, range(2, KB))
                if f is not None:
                    pe.wait_ge(kst_ok, 4 * f + 3)
                    rows_max(f, 0, W0)
                if b is not None:
                    values(b, 4)
                if l is not None:
                    pe.wait_ge(x2n_ok, l + 1)
                    if f is not None:
                        pe.wait_ge(qst_ok, 4 * f + 3)
                    for k in range(KB):
                        m = turn(W1[:, k * P:(k + 1) * P], x2n[:, k * P:(k + 1) * P])
                    m.then_inc(x2T_ps, 1)
                if a is not None:
                    project(W2, DM, xTH, xTL, Q0, range(2, KB))
                    add_bias(W2, DM, BQ).then_inc(q_ps, 1)
                if b is not None:
                    values(b, 5)
                if f is not None:
                    pe.wait_ge(mrows, 4 * f + 1)
                    stack_k(3)
                    if l is not None:
                        pe.wait_ge(x2L_ok, l + 1)
                    else:
                        pe.wait_ge(qst_ok, 4 * f + 3)
                    stack_q(3)
                if last(i):
                    g_or_u(0, 0, 0, 1, range(2))
                if f is not None:
                    scores(f, 2)
                if a is not None:
                    pe.wait_ge(ctL_ok, a + 1)
                    if f is not None:
                        pe.wait_ge(kst_ok, 4 * f + 4)
                    project(W0, 2 * KVD, ctH, ctL, KV0, range(2))
                    project(W0, 2 * KVD, ctH, ctL, KV0, range(2, KB))
                    add_bias(W0, 2 * KVD, BK).then_inc(kv_ps, 1)

            attention(pe, step)

            def gu(c, s, h):
                pe.wait_ge(w13L_ok, c + 1)
                need(pe, h_ok, c - 1)
                g_or_u(c, s, h, 0)
                g_or_u(c, s, h, 1)

            def y(c, s, start, stop):
                pe.wait_ge(hL_ok, c + 1)
                pe.wait_ge(w2L_ok, c + 1)
                for t in range(HT):
                    w = slice(t * P, (t + 1) * P)
                    m = three(Y[t], hH[:, s, w], hL[:, s, w], w2H[:, s, :], w2L[:, s, :], start, stop)
                    if stop:
                        m.then_inc(y_ps, 1)
                if not stop:
                    m.then_inc(y_used, 1)

            l = NBATCH - 1
            values(l, 6)
            values(l, 7)
            g_or_u(0, 0, 0, 1, range(2, KB))
            pe.wait_ge(on_ok, 4 * NBATCH)
            pe.wait_ge(x2L_ok, l)
            turn4(W1, on[:].rearrange("p h d -> p (h d)")).then_inc(aT_ps, 1)
            pe.wait_ge(w13L_ok, 2)
            pe.wait_ge(mrows, 4 * NBATCH)
            g_or_u(1, 1, 0, 0, range(2))
            pe.wait_ge(aTL_ok, NBATCH)
            pe.wait_ge(x2_ok, l)
            project(W2, DM, aTH, aTL, O0, range(KB))
            add_bias(W2, DM, BO).then_inc(o_ps, 1)
            g_or_u(1, 1, 0, 0, range(2, KB))
            pe.wait_ge(x2_ok, NBATCH)
            g_or_u(1, 1, 0, 1)
            pe.wait_ge(x2n_ok, NBATCH)
            turn4(W1, x2n).then_inc(x2T_ps, 1)
            gu(2, 0, 0)
            pe.wait_ge(exp_ok, 2 * KVH * NBATCH)
            pe.wait_ge(x2L_ok, NBATCH)
            y(0, 0, True, False)
            y(1, 1, False, False)
            gu(3, 1, 0)
            y(2, 0, False, False)

            for h in range(HALVES):
                c = h * NCH
                if h:
                    gu(c, 0, h)
                    y(c - 1, 1, False, True)
                    gu(c + 1, 1, h)
                    pe.wait_ge(fin_ok, h * HT)
                    y(c, 0, True, False)
                with pe.Fori(1 if h else 2, NCH // 2) as p:
                    gu(c + 2 * p, 0, h)
                    y(c + 2 * p - 1, 1, False, False)
                    gu(c + 2 * p + 1, 1, h)
                    y(c + 2 * p, 0, False, False)
            y(CHUNKS - 1, 1, False, True)


def kernel(**inputs):
    import numpy as np
    import concourse.bacc as bacc
    from concourse.bass_utils import run_bass_kernel_spmd

    f = {k: np.asarray(v) for k, v in inputs.items()}
    ctxt = f["ctx_4096"].reshape(NBATCH, P, KB, P).transpose(0, 3, 2, 1).reshape(NBATCH, P, DM)

    def rows(w):
        return w.reshape(KB, P, w.shape[1]).transpose(1, 0, 2).reshape(P, -1)

    def pairs(w):
        return w.reshape(-1, PAIRS, 2, GJ, DH).transpose(0, 1, 3, 2, 4).reshape(-1, DM)

    wkv = np.concatenate([f["L0_xattn_Wk"], f["L0_xattn_Wv"]], axis=1)
    wproj = np.concatenate([rows(wkv), rows(pairs(f["L0_xattn_Wq"])), rows(f["L0_xattn_Wo"])], axis=1)
    w1, w3 = (f[n].reshape(NCH, P, KB, P).transpose(0, 3, 2, 1).reshape(NCH, P, DM) for n in ("L0_ffn_w1", "L0_ffn_w3"))
    w2 = f["L0_ffn_w2"].reshape(DM, NCH, P).transpose(1, 2, 0)
    wff = np.concatenate([w1, w3, w2], axis=2)
    scales = np.concatenate([f["L0_ffn_w1_scale"], f["L0_ffn_w3_scale"], f["L0_ffn_w2_scale"].T], axis=1)
    small = np.concatenate([pairs(f["L0_xattn_bq"][None])[0], f["L0_xattn_bk"], f["L0_xattn_bv"], f["L0_xattn_bo"],
                            f["g_xattn"], f["g_ffn"], scales.reshape(-1)])[None]

    nc = bacc.Bacc("TRN2", target_bir_lowering=False, num_devices=1)
    arrays = {"x": f["x"], "ctxt": ctxt, "wproj": wproj, "small": small, "wff": wff}
    arrays = {k: np.ascontiguousarray(v) for k, v in arrays.items()}
    args = [nc.dram_tensor("in_" + k, v.shape, F32, kind="ExternalInput").ap() for k, v in arrays.items()]
    out = nc.dram_tensor("out", arrays["x"].shape, F32, kind="ExternalOutput").ap()
    build(nc, *args, out)
    r = run_bass_kernel_spmd(nc, [{"in_" + k: v for k, v in arrays.items()}], core_ids=[0])
    return r.results[0]["out"]
```
